# Optimizing a Trainium2 kernel written in Bass

```python
import numpy as np
import jax
import jax.numpy as jnp

def _softmax(x, axis=-1):
    return jax.nn.softmax(x, axis=axis)

def _gelu(x):
    return jax.nn.gelu(x, approximate=True)

def _silu(x):
    return jax.nn.silu(x)

def _sigmoid(x):
    return jax.nn.sigmoid(x)

def _layernorm(x, axis=-1, eps=1e-05):
    m = jnp.mean(x, axis=axis, keepdims=True)
    v = jnp.var(x, axis=axis, keepdims=True)
    return (x - m) / jnp.sqrt(v + eps)

def _scatter_add(tgt, idx, src, axis=0):
    return tgt.at[idx].add(src)

def _segment_sum(src, seg, n):
    return jax.ops.segment_sum(src, seg, n)
kernel_name = 'mk_adj_resnorm_d2_adj_r2_8524ec'

def setup_inputs(seed: int=0):
    np.random.seed(seed)
    _w = jnp.asarray

    def _rec_inputs():
        import jax
        import jax.numpy as jnp
        _gk = jax.random.key(seed)
        x = -0.0002928 + 1 * jax.random.normal(jax.random.fold_in(_gk, 1), (4096, 256), jnp.float32)
        _a = jax.random.bernoulli(jax.random.fold_in(_gk, 2), 0.00390625, (4096, 4096))
        _a = jnp.logical_or(_a, jnp.swapaxes(_a, -1, -2))
        _a = jnp.logical_or(_a, jnp.eye(4096, dtype=bool))
        _af = _a.astype(jnp.float32)
        adj = _af
        return (x, adj)
    x, adj = _rec_inputs()

    def _L0_gnn_setup():
        import jax, jax.numpy as jnp
        import numpy as np
        N = 4096
        D_IN = 256
        D_OUT = 256
        NEG_BIG = -9000000000000000.0
        key = jax.random.key(seed)
        kx, ka, kw, kb, kn, ke = jax.random.split(key, 6)
        x = jax.random.normal(kx, (N, D_IN), dtype=jnp.float32)
        adj = (jax.random.uniform(ka, (N, N)) > 0.9).astype(jnp.float32)
        stdv = 1.0 / np.sqrt(D_OUT)
        weight = jax.random.uniform(kw, (D_IN, D_OUT), minval=-stdv, maxval=stdv, dtype=jnp.float32)
        bias = jax.random.uniform(kb, (D_OUT,), minval=-stdv, maxval=stdv, dtype=jnp.float32)
        node_w = jax.random.uniform(kn, (D_IN, 1), minval=-1.0, maxval=1.0, dtype=jnp.float32)
        stdv_e = 1.0 / np.sqrt(D_IN)
        edge_w = jax.random.uniform(ke, (D_IN, D_IN), minval=-stdv_e, maxval=stdv_e, dtype=jnp.float32)
        return {'x': x, 'adj': adj, 'weight': weight, 'bias': bias, 'node_w': node_w, 'edge_w': edge_w}
    _L0_gnn_all = _L0_gnn_setup()
    _L0_gnn_in = {k: v for k, v in _L0_gnn_all.items() if k in ('weight', 'bias', 'node_w', 'edge_w')}
    del _L0_gnn_all

    def _L1_gnn_setup():
        import jax, jax.numpy as jnp
        import numpy as np
        N, NIN, NOUT = (4096, 256, 256)
        key = jax.random.key(seed)
        k1, k2, k3 = jax.random.split(key, 3)
        H = jax.random.normal(k1, (N, NIN), dtype=jnp.float32)
        adj_matrix = jax.random.uniform(k2, (N, N), dtype=jnp.float32)
        W = jax.random.normal(k3, (NOUT, NIN), dtype=jnp.float32) / np.sqrt(NIN)
        b = jnp.zeros((NOUT,), dtype=jnp.float32)
        return {'H': H, 'adj_matrix': adj_matrix, 'W': W, 'b': b}
    _L1_gnn_all = _L1_gnn_setup()
    _L1_gnn_in = {k: v for k, v in _L1_gnn_all.items() if k in ('W', 'b')}
    del _L1_gnn_all
    return {'x': x, 'adj': adj, 'L0_gnn_weight': _L0_gnn_in['weight'], 'L0_gnn_bias': _L0_gnn_in['bias'], 'L0_gnn_node_w': _L0_gnn_in['node_w'], 'L0_gnn_edge_w': _L0_gnn_in['edge_w'], 'L1_gnn_W': _L1_gnn_in['W'], 'L1_gnn_b': _L1_gnn_in['b']}

def reference(x, adj, L0_gnn_weight, L0_gnn_bias, L0_gnn_node_w, L0_gnn_edge_w, L1_gnn_W, L1_gnn_b):
    import jax
    import jax.numpy as jnp

    def _L0_gnn_ref(x, adj, weight, bias, node_w, edge_w):
        import jax, jax.numpy as jnp
        import numpy as np
        N = 4096
        D_IN = 256
        D_OUT = 256
        NEG_BIG = -9000000000000000.0
        node_att = jax.nn.softmax(x @ node_w, axis=0)
        h = x @ edge_w
        e = h @ h.T
        e = jnp.where(adj > 0, e, NEG_BIG)
        edge_att = jax.nn.softmax(e, axis=1)
        combined_att = node_att * edge_att
        support = x @ weight
        output = adj * combined_att @ support
        return output + bias

    def _L1_gnn_ref(H, adj_matrix, W, b):
        import jax, jax.numpy as jnp
        import numpy as np
        N, NIN, NOUT = (4096, 256, 256)
        n = adj_matrix.shape[0]
        A = adj_matrix + jnp.eye(n, dtype=adj_matrix.dtype)
        deg = jnp.sum(A, axis=0)
        d = deg ** (-0.5)
        d = jnp.where(jnp.isinf(d), 0.0, d)
        A = d[:, None] * A * d[None, :]
        Hm = A @ H
        out = jnp.tanh(Hm @ W.T + b)
        return out
    x = _layernorm(x + _L0_gnn_ref(x, adj, L0_gnn_weight, L0_gnn_bias, L0_gnn_node_w, L0_gnn_edge_w), axis=-1)
    x = _layernorm(x + _L1_gnn_ref(x, adj, L1_gnn_W, L1_gnn_b), axis=-1)
    return x

_drawn_inputs = setup_inputs


def setup_inputs(seed=0):
    import zlib

    import numpy as np

    out = dict(_drawn_inputs(seed))
    spreads = {'L1_gnn_b': (0.0, 0.1)}
    factors = {'L0_gnn_weight': 108.49, 'L0_gnn_node_w': 62.425}
    for name, (base, spread) in spreads.items():
        noise = np.random.default_rng([zlib.crc32(name.encode()), seed]).standard_normal(out[name].shape)
        drawn = base * np.exp(spread * noise) if base else spread * noise
        out[name] = jnp.asarray(drawn.astype(out[name].dtype))
    for name, factor in factors.items():
        out[name] = (out[name] * factor).astype(out[name].dtype)
    return out
```

```python
from contextlib import ExitStack

import concourse.bass as bass
from concourse import mybir

P = 128
ALU = mybir.AluOpType
ACT = mybir.ActivationFunctionType
AX = mybir.AxisListType
F32 = mybir.dt.float32
I32 = mybir.dt.int32
RMAX = bass.bass_isa.ReduceOp.max
RADD = bass.bass_isa.ReduceOp.add

NEG_BIG = -9000000000000000.0
EPS = 1e-5
RSQRT_SEED = 0x5F3759DF
RSQRT_STEPS = 3


def general_path(nc, x, adj, w0, b0, node_w, edge_w, w1, b1, out):
    N, D = x.shape
    NB = N // P
    KD = D // P
    CH = 512
    UN = CH
    U = N // UN
    C = N // CH
    TJ = CH // P
    GR = CH // P
    NG = NB // GR

    with ExitStack() as ctx:
        def sb(name, shape, dt=F32):
            return ctx.enter_context(nc.sbuf_tensor(name, shape, dt))

        def psum(name, shape, dt=F32):
            return ctx.enter_context(nc.psum_tensor(name, shape, dt))

        def sem(name):
            return ctx.enter_context(nc.semaphore(name))

        hT = sb("hT", [P, KD, N])
        sup = sb("sup", [P, NB, D])
        x1 = sb("x1", [P, NB, D])
        A = sb("A", [P, 2, N])
        M = sb("M", [P, 2, N])
        colsum = sb("colsum", [P, N])
        negs = sb("negs", [P, 2, CH])
        PT = sb("PT", [P, 4, CH])
        hI = sb("hI", [P, 2, KD, P])
        edge_sb = sb("edge_sb", [P, KD, D])
        w0n = sb("w0n", [P, KD, D + 1])
        w1T = sb("w1T", [P, KD, D])
        b0_sb = sb("b0_sb", [P, D])
        b1_sb = sb("b1_sb", [P, D])
        ident = sb("ident", [P, P])
        ones = sb("ones", [P, P])
        logits = sb("logits", [P, NB])
        att = sb("att", [P, NB])
        small = sb("small", [P, 8])
        unitmax = sb("unitmax", [P, U])
        negmax = sb("negmax", [P, 2])
        unitsum = sb("unitsum", [P, 2, U])
        rowscale = sb("rowscale", [P, 4])
        stats = sb("stats", [P, 6])
        meanvar = sb("meanvar", [P, 2])
        nv = sb("nv", [P, NB])
        ny = sb("ny", [P, NB])
        nt = sb("nt", [P, NB])
        dinv = sb("dinv", [P, NB])
        scratch = sb("scratch", [P, 1])
        y = sb("y", [P, D])
        hm = sb("hm", [P, D])
        hmT = sb("hmT", [P, KD, P])
        th = sb("th", [P, D])
        obuf = sb("obuf", [P, 2, D])
        w1_sb = obuf
        b0_row, b1_row = y[0:1, :], hm[0:1, :]
        xg = [A[:, b, 0:GR * D].rearrange("p (r d) -> p r d", r=GR) for b in range(2)]
        xT = [M[:, b, 0:KD * CH].rearrange("p (k n) -> p k n", k=KD) for b in range(2)]

        E4 = psum("E4", [P, 4 * CH])
        E = [E4[:, i * CH:(i + 1) * CH] for i in range(4)]
        EA, EB = E4[:, 0:2 * CH], E4[:, 2 * CH:4 * CH]
        T = [psum(f"T{i}", [P, CH]) for i in range(2)]
        O = [psum(f"O{i}", [P, CH]) for i in range(2)]
        S4 = T + O

        w_loaded = sem("w_loaded")
        x1_loaded = sem("x1_loaded")
        xg_loaded = [sem(f"xg_loaded{i}") for i in range(2)]
        a_loaded = [sem(f"a_loaded{i}") for i in range(2)]
        ident_zero = sem("ident_zero")
        consts = sem("consts")
        bias_ready = sem("bias_ready")
        bias_copied = sem("bias_copied")
        wt_ready = sem("wt_ready")
        wt_copied = sem("wt_copied")
        xt_ready = sem("xt_ready")
        xt_copied_act = sem("xt_copied_act")
        xt_copied_dve = sem("xt_copied_dve")
        h_ready = sem("h_ready")
        h_copied = sem("h_copied")
        sup_ready = sem("sup_ready")
        sup_copied = sem("sup_copied")
        node_dve = sem("node_dve")
        node_pool = sem("node_pool")
        node_act = sem("node_act")
        att_ready = sem("att_ready")
        hi_staged = sem("hi_staged")
        x_biased = sem("x_biased")
        a_summed = sem("a_summed")
        a_used = sem("a_used")
        e_ready = sem("e_ready")
        e_masked = sem("e_masked")
        negmax_ready = sem("negmax_ready")
        exp_done = sem("exp_done")
        p_ready = sem("p_ready")
        t_ready = sem("t_ready")
        t_copied = sem("t_copied")
        pv_done = sem("pv_done")
        o_read = sem("o_read")
        deg_ready = sem("deg_ready")
        g_ready = sem("g_ready")
        hm_ready = sem("hm_ready")
        hmt_ready = sem("hmt_ready")
        hmt_copied = sem("hmt_copied")
        lin_ready = sem("lin_ready")
        lin_biased = sem("lin_biased")
        tanh_done = sem("tanh_done")
        y_ready = sem("y_ready")
        stored = [sem(f"stored{i}") for i in range(2)]
        dve_chain = sem("dve_chain")

        x_groups = x.rearrange("(g r p) d -> g p r d", p=P, r=GR)
        x_rows = x.rearrange("(b p) d -> p b d", p=P)
        adj_rows = adj.rearrange("(b p) n -> b p n", p=P)
        out_rows = out.rearrange("(b p) d -> b p d", p=P)

        block = ctx.enter_context(nc.Block())

        @block.sync
        def _(sp):
            sp.dma_start(edge_sb[:, :, :], edge_w.rearrange("(k p) d -> p k d", p=P)).then_inc(w_loaded, 16)
            sp.dma_start(w0n[:, :, 0:D], w0.rearrange("(k p) d -> p k d", p=P)).then_inc(w_loaded, 16)
            sp.dma_start(w0n[:, :, D:D + 1], node_w.rearrange("(k p) d -> p k d", p=P),
                         allow_slow_non_contiguous=True).then_inc(w_loaded, 16)
            sp.dma_start(w1_sb[:, :, :], w1.rearrange("(k p) d -> p k d", p=P)).then_inc(w_loaded, 16)
            sp.dma_start(b0_row[:, :], b0.rearrange("(a d) -> a d", a=1)).then_inc(w_loaded, 16)
            sp.dma_start(b1_row[:, :], b1.rearrange("(a d) -> a d", a=1)).then_inc(w_loaded, 16)
            for g in range(2):
                sp.dma_start(xg[g], x_groups[g]).then_inc(xg_loaded[g], 16)
            with sp.Fori(2, NG - 1, 2) as g0:
                for b in range(2):
                    g = g0 + b
                    sp.wait_ge(xt_ready, g - 1)
                    sp.dma_start(xg[b], x_groups[bass.ds(g, 1)].rearrange("a p r d -> (a p) r d")
                                 ).then_inc(xg_loaded[b], 16)
            sp.dma_start(x1[:, :, :], x_rows).then_inc(x1_loaded, 16)
            sp.wait_ge(xt_ready, NG)
            for b in range(2):
                sp.dma_start(A[:, b, :], adj_rows[b]).then_inc(a_loaded[b], 16)
            with sp.Fori(2, NB - 1, 2) as i0:
                for b in range(2):
                    i = i0 + b
                    sp.wait_ge(a_used, i - 1)
                    sp.wait_ge(a_summed, i - 1)
                    sp.dma_start(A[:, b, :], adj_rows[bass.ds(i, 1)].rearrange("a p n -> (a p) n")
                                 ).then_inc(a_loaded[b], 16)
            for b in range(2):
                sp.wait_ge(a_used, NB - 1 + b)
                sp.wait_ge(a_summed, NB - 1 + b)
                sp.dma_start(A[:, b, :], adj_rows[b]).then_inc(a_loaded[b], 16)
            with sp.Fori(0, NB - 3, 2) as j0:
                for b in range(2):
                    j = j0 + b
                    sp.wait_ge(t_ready, C * (NB + 1) + C * j)
                    sp.dma_start(A[:, b, :], adj_rows[bass.ds(j + 2, 1)].rearrange("a p n -> (a p) n")
                                 ).then_inc(a_loaded[b], 16)
                    sp.wait_ge(y_ready, j + 1)
                    sp.dma_start(out_rows[bass.ds(j, 1)].rearrange("a p d -> (a p) d"), obuf[:, b, :]
                                 ).then_inc(stored[b], 16)
            for b in range(2):
                sp.wait_ge(y_ready, NB - 1 + b)
                sp.dma_start(out_rows[NB - 2 + b], obuf[:, b, :]).then_inc(stored[b], 16)
            for b in range(2):
                sp.wait_ge(stored[b], 16 * (NB // 2))

        @block.tensor
        def _(pe):
            pe.wait_ge(consts, 3)
            pe.wait_ge(w_loaded, 96)
            nc.tensor.matmul(O[0][:, 0:D], ones[0:1, :], b0_row[:, :], start=True, stop=True)
            nc.tensor.matmul(O[1][:, 0:D], ones[0:1, :], b1_row[:, :], start=True, stop=True
                             ).then_inc(bias_ready, 1)
            for k in range(KD):
                for o in range(KD):
                    last = nc.tensor.transpose(T[0][:, (k * KD + o) * P:(k * KD + o + 1) * P],
                                               w1_sb[:, o, k * P:(k + 1) * P], ident[:, :])
            last.then_inc(wt_ready, 1)

            def transpose_group(g, b):
                pe.wait_ge(xg_loaded[b], 8 * (g - b) + 16)
                for k in range(KD):
                    for r in range(GR):
                        last = nc.tensor.transpose(EA[:, k * CH + r * P:k * CH + (r + 1) * P],
                                                   xg[b][:, r, k * P:(k + 1) * P], ident[:, :])
                last.then_inc(xt_ready, 1)

            def project_group(g, b, first=False):
                pe.wait_ge(xt_copied_act, g + 1)
                pe.wait_ge(xt_copied_dve, g + 1)
                if not first:
                    pe.wait_ge(h_copied, g)
                for m in range(KD):
                    for k in range(KD):
                        last = nc.tensor.matmul(EB[:, m * CH:(m + 1) * CH], edge_sb[:, k, m * P:(m + 1) * P],
                                                xT[b][:, k, :], start=(k == 0), stop=(k == KD - 1))
                last.then_inc(h_ready, 1)
                if not first:
                    pe.wait_ge(sup_copied, g)
                for r in range(GR):
                    for k in range(KD):
                        last = nc.tensor.matmul(S4[r][:, 0:D + 1], xT[b][:, k, r * P:(r + 1) * P], w0n[:, k, :],
                                                start=(k == 0), stop=(k == KD - 1))
                last.then_inc(sup_ready, 1)

            def next_transpose(g, b):
                pe.wait_ge(xt_copied_act, g)
                pe.wait_ge(xt_copied_dve, g)
                transpose_group(g, b)

            transpose_group(0, 0)
            pe.wait_ge(bias_copied, 1)
            pe.wait_ge(wt_copied, 1)
            next_transpose(1, 1)
            project_group(0, 0, first=True)
            next_transpose(2, 0)
            project_group(1, 1)
            with pe.Fori(2, NG - 3, 2) as g0:
                for b in range(2):
                    next_transpose(g0 + b + 1, (b + 1) % 2)
                    project_group(g0 + b, b)
            next_transpose(NG - 1, 1)
            project_group(NG - 2, 0)
            project_group(NG - 1, 1)

            def scores(i, b, first=False):
                pe.wait_ge(hi_staged, i + 1)
                for u in range(U):
                    if not (first and u < 4):
                        pe.wait_ge(e_masked, U * i + u - 3)
                    for k in range(KD):
                        last = nc.tensor.matmul(E[u % 4], hI[:, b, k, :], hT[:, k, u * UN:(u + 1) * UN],
                                                start=(k == 0), stop=(k == KD - 1))
                    last.then_inc(e_ready, 1)

            def transpose_chunk(n, c, src, first=False):
                if not (first and c < 2):
                    pe.wait_ge(t_copied, C * n + c - 1)
                for t in range(TJ):
                    col = c * CH + t * P
                    last = nc.tensor.transpose(T[c % 2][:, t * P:(t + 1) * P], src[:, col:col + P], ident[:, :])
                last.then_inc(t_ready, 1)

            def product_chunk(n, b, c):
                pe.wait_ge(t_copied, C * n + c + 1)
                for t in range(TJ):
                    last = nc.tensor.matmul(O[b][:, 0:D], PT[:, c % 4, t * P:(t + 1) * P], sup[:, c * TJ + t, :],
                                            start=(c == 0 and t == 0), stop=(c == C - 1 and t == TJ - 1))
                last.then_inc(pv_done, 1)

            def attend(i, b, first=False):
                for c in range(C):
                    pe.wait_ge(p_ready, U * i + c + 1)
                    transpose_chunk(i, c, M[:, b, :], first)
                    if c == 1 and not first:
                        pe.wait_ge(o_read, i - 1)
                    if c > 0:
                        product_chunk(i, b, c - 1)
                product_chunk(i, b, C - 1)

            pe.wait_ge(h_copied, NG)
            pe.wait_ge(sup_copied, NG)
            scores(0, 0, first=True)
            scores(1, 1)
            attend(0, 0, first=True)
            scores(2, 0)
            attend(1, 1)
            with pe.Fori(2, NB - 3, 2) as i0:
                for b in range(2):
                    scores(i0 + b + 1, (b + 1) % 2)
                    attend(i0 + b, b)
            scores(NB - 1, 1)
            attend(NB - 2, 0)
            attend(NB - 1, 1)

            pe.wait_ge(a_summed, NB)
            for t in range(NB):
                last = nc.tensor.matmul(E[0][:, t:t + 1], colsum[:, t * P:(t + 1) * P], ones[:, 0:1],
                                        start=True, stop=True)
            last.then_inc(deg_ready, 1)

            def hm_transpose(j):
                pe.wait_ge(hm_ready, j + 1)
                for k in range(KD):
                    last = nc.tensor.transpose(E[0][:, k * P:(k + 1) * P], hm[:, k * P:(k + 1) * P], ident[:, :])
                last.then_inc(hmt_ready, 1)

            def hm_linear(j):
                pe.wait_ge(hmt_copied, j + 1)
                pe.wait_ge(lin_biased, j)
                for k in range(KD):
                    last = nc.tensor.matmul(E[1][:, 0:D], hmT[:, k, :], w1T[:, k, :],
                                            start=(k == 0), stop=(k == KD - 1))
                last.then_inc(lin_ready, 1)

            def aggregate(j, b, first=False):
                n = NB + j
                pe.wait_ge(a_loaded[b], 16 * (NB // 2) + 8 * (j - b) + 16)
                for c in range(C):
                    transpose_chunk(n, c, A[:, b, :])
                    if c == 1:
                        pe.wait_ge(o_read, n - 1)
                    if c > 0:
                        if first:
                            pe.wait_ge(g_ready, TJ * c)
                        product_chunk(n, b, c - 1)
                    if c == 3 and not first:
                        hm_transpose(j - 1)
                    if c == 5 and not first:
                        hm_linear(j - 1)
                if first:
                    pe.wait_ge(g_ready, NB)
                product_chunk(n, b, C - 1)

            aggregate(0, 0, first=True)
            aggregate(1, 1)
            with pe.Fori(2, NB - 1, 2) as j0:
                for b in range(2):
                    aggregate(j0 + b, b)
            hm_transpose(NB - 1)
            hm_linear(NB - 1)

        @block.gpsimd
        def _(pool):
            nc.gpsimd.memset(ident[:, :], 0.0).then_inc(ident_zero, 1)
            nc.gpsimd.memset(ones[:, :], 1.0).then_inc(consts, 1)
            pool.wait_ge(ident_zero, 1)
            nc.gpsimd.affine_select(out=ident[:, :], in_=ident[:, :], compare_op=ALU.not_equal, fill=1.0, base=0,
                                    pattern=[[-1, P]], channel_multiplier=1).then_inc(consts, 1)
            nc.gpsimd.memset(colsum[:, :], 0.0).then_inc(consts, 1)
            pool.wait_ge(bias_copied, 1)
            pool.wait_ge(x1_loaded, 16)
            pool.wait_ge(h_copied, NG)

            def stage(i, b):
                nc.gpsimd.tensor_copy(hI[:, b, :, :], hT[:, :, bass.ds(i * P, P)]).then_inc(hi_staged, 1)

            def add_bias(i):
                nc.gpsimd.tensor_tensor(x1[:, bass.ds(i, 1), :].rearrange("p a d -> p (a d)"),
                                        x1[:, bass.ds(i, 1), :].rearrange("p a d -> p (a d)"), b0_sb[:, :],
                                        ALU.add).then_inc(x_biased, 1)

            def add_columns(i, b, first=False):
                pool.wait_ge(a_loaded[b], 8 * (i - b) + 16)
                if not first:
                    pool.wait_ge(a_summed, i)
                nc.gpsimd.tensor_tensor(colsum[:, :], colsum[:, :], A[:, b, :], ALU.add).then_inc(a_summed, 1)

            stage(0, 0)
            stage(1, 1)
            pool.wait_ge(node_dve, 1)
            nc.gpsimd.partition_all_reduce(small[:, 1:2], small[:, 0:1], P, RMAX).then_inc(node_pool, 1)
            pool.wait_ge(node_act, 1)
            nc.gpsimd.partition_all_reduce(small[:, 4:5], small[:, 3:4], P, RADD).then_inc(node_pool, 1)
            pool.wait_ge(consts, 3)
            add_bias(0)
            add_columns(0, 0, first=True)
            add_bias(1)
            add_columns(1, 1)
            with pool.Fori(2, NB - 1, 2) as i0:
                for b in range(2):
                    i = i0 + b
                    pool.wait_ge(e_ready, U * (i - 1))
                    stage(i, b)
                    add_bias(i)
                    add_columns(i, b)

        @block.scalar
        def _(act):
            act.wait_ge(bias_ready, 1)
            nc.scalar.copy(b0_sb[:, :], O[0][:, 0:D])
            nc.scalar.copy(b1_sb[:, :], O[1][:, 0:D]).then_inc(bias_copied, 1)
            act.wait_ge(wt_ready, 1)
            nc.scalar.copy(w1T[:, :, :], T[0][:, :].rearrange("p (k n) -> p k n", k=KD)).then_inc(wt_copied, 1)

            def copy_group(g, b, first=False):
                act.wait_ge(xt_ready, g + 1)
                if not first:
                    act.wait_ge(sup_ready, g - 1)
                nc.scalar.copy(xT[b][:, 0, :], EA[:, 0:CH]).then_inc(xt_copied_act, 1)

            def copy_h(g):
                act.wait_ge(h_ready, g + 1)
                nc.scalar.copy(hT[:, :, bass.ds(g * CH, CH)], EB.rearrange("p (k n) -> p k n", k=KD)
                               ).then_inc(h_copied, 1)

            copy_group(0, 0, first=True)
            copy_group(1, 1, first=True)
            with act.Fori(0, NG - 3, 2) as g0:
                for b in range(2):
                    copy_h(g0 + b)
                    copy_group(g0 + b + 2, b)
            copy_h(NG - 2)
            copy_h(NG - 1)
            act.wait_ge(node_dve, 2)
            nc.scalar.activation(att[:, :], logits[:, :], ACT.Exp, bias=small[:, 2:3], scale=1.0,
                                 accum_out=small[:, 3:4]).then_inc(node_act, 1)

            def exps(i, b, u):
                if u == 0:
                    act.wait_ge(negmax_ready, i + 1)
                nc.scalar.activation(M[:, b, u * UN:(u + 1) * UN], M[:, b, u * UN:(u + 1) * UN], ACT.Exp,
                                     bias=negmax[:, b:b + 1], scale=1.0,
                                     accum_out=unitsum[:, b, u:u + 1]).then_inc(exp_done, 1)

            def copy_transposed(n, c, first=False):
                act.wait_ge(t_ready, C * n + c + 1)
                if not (first and c < 4):
                    act.wait_ge(pv_done, C * n + c - 3)
                nc.scalar.copy(PT[:, c % 4, :], T[c % 2][:, :]).then_inc(t_copied, 1)

            def attend(i, b, first=False, last=False):
                for c in range(C):
                    copy_transposed(i, c, first)
                    if not last:
                        exps(i + 1, (b + 1) % 2, c)

            for u in range(U):
                exps(0, 0, u)
            attend(0, 0, first=True)
            attend(1, 1)
            with act.Fori(2, NB - 3, 2) as i0:
                for b in range(2):
                    attend(i0 + b, b)
            attend(NB - 2, 0)
            attend(NB - 1, 1, last=True)

            def aggregate(j, first=False):
                for c in range(C):
                    copy_transposed(NB + j, c)
                    if c == 4 and not first:
                        copy_hmT(j - 1)
                    if c == 7 and not first:
                        tanh(j - 1)

            def copy_hmT(j):
                act.wait_ge(hmt_ready, j + 1)
                nc.scalar.copy(hmT[:, :, :], E[0][:, 0:D].rearrange("p (k n) -> p k n", k=KD)
                               ).then_inc(hmt_copied, 1)

            def tanh(j):
                act.wait_ge(lin_biased, j + 1)
                nc.scalar.activation(th[:, :], th[:, :], ACT.Tanh).then_inc(tanh_done, 1)

            aggregate(0, first=True)
            with act.Fori(1, NB, 1) as j:
                aggregate(j)
            copy_hmT(NB - 1)
            tanh(NB - 1)

        @block.vector
        def _(dve):
            links = [0]

            def link(ins):
                links[0] = links[0] + 1
                ins.then_inc(dve_chain, 1)
                dve.wait_ge(dve_chain, links[0])

            def carry_wait():
                nc.vector.memset(scratch[:, :], 0.0)

            def rsqrt(v, r, t):
                link(nc.vector.tensor_scalar(r.bitcast(I32), v.bitcast(I32), -0.5, float(RSQRT_SEED),
                                             ALU.mult, ALU.add))
                for _ in range(RSQRT_STEPS):
                    link(nc.vector.scalar_tensor_tensor(out=t, in0=r, scalar=-0.5, in1=r, op0=ALU.mult,
                                                        op1=ALU.mult))
                    link(nc.vector.tensor_tensor(t, t, v, ALU.mult))
                    link(nc.vector.scalar_tensor_tensor(out=r, in0=t, scalar=1.5, in1=r, op0=ALU.add,
                                                        op1=ALU.mult))

            def copy_group(g, b, first=False):
                dve.wait_ge(xt_ready, g + 1)
                if not first:
                    dve.wait_ge(sup_ready, g - 1)
                nc.vector.tensor_copy(xT[b][:, 1, :], EA[:, CH:2 * CH]).then_inc(xt_copied_dve, 1)

            def copy_support(g):
                dve.wait_ge(sup_ready, g + 1)
                for r in range(GR):
                    nc.vector.tensor_copy(sup[:, bass.ds(g * GR + r, 1), :].rearrange("p a d -> p (a d)"),
                                          S4[r][:, 0:D])
                    last = nc.vector.tensor_copy(logits[:, bass.ds(g * GR + r, 1)], S4[r][:, D:D + 1])
                last.then_inc(sup_copied, 1)

            copy_group(0, 0, first=True)
            copy_group(1, 1, first=True)
            with dve.Fori(0, NG - 3, 2) as g0:
                for b in range(2):
                    copy_support(g0 + b)
                    copy_group(g0 + b + 2, b)
            copy_support(NG - 2)
            copy_support(NG - 1)

            def mask_and_max(i, b):
                dve.wait_ge(a_loaded[b], 8 * (i - b) + 16)
                def mask(u):
                    return nc.vector.tensor_scalar(negs[:, u % 2, :], A[:, b, u * UN:(u + 1) * UN], 0.0, NEG_BIG,
                                                   ALU.is_le, ALU.mult)

                dve.wait_ge(e_masked, U * i)
                ins = mask(0)
                for u in range(U):
                    link(ins)
                    dve.wait_ge(e_ready, U * i + u + 1)
                    dve.wait_ge(e_masked, U * i + u)
                    if u + 1 < U:
                        ins = mask(u + 1)
                    else:
                        carry_wait()
                    nc.vector.tensor_tensor_reduce(
                        out=M[:, b, u * UN:(u + 1) * UN], in0=E[u % 4], in1=negs[:, u % 2, :], scale=1.0,
                        scalar=-3.0e38, op0=ALU.add, op1=ALU.max, accum_out=unitmax[:, u:u + 1]
                    ).then_inc(e_masked, 1)
                dve.wait_ge(e_masked, U * i + U)
                nc.vector.tensor_reduce(negmax[:, b:b + 1], unitmax[:, :], AX.X, ALU.max, negate=True
                                        ).then_inc(negmax_ready, 1)

            def weigh(i, b):
                for u in range(U):
                    dve.wait_ge(exp_done, U * i + u + 1)
                    cols = slice(u * UN, (u + 1) * UN)
                    ins = nc.vector.tensor_tensor(M[:, b, cols], M[:, b, cols], A[:, b, cols], ALU.mult)
                    ins.then_inc(p_ready, 1)
                dve.wait_ge(p_ready, U * i + U)
                nc.vector.sem_inc(a_used, 1)

            def normalise(dst):
                link(nc.vector.bn_stats(stats[:, :], y[:, :]))
                carry_wait()
                link(nc.vector.bn_aggr(meanvar[:, :], stats[:, :]))
                link(nc.vector.tensor_scalar(nv[:, 0:1], meanvar[:, 1:2], EPS, None, ALU.add))
                rsqrt(nv[:, 0:1], ny[:, 0:1], nt[:, 0:1])
                return nc.vector.tensor_scalar(dst, y[:, :], meanvar[:, 0:1], ny[:, 0:1], ALU.subtract, ALU.mult)

            def finish_first(i, b):
                link(nc.vector.tensor_reduce(rowscale[:, 0:1], unitsum[:, b, :], AX.X, ALU.add))
                link(nc.vector.reciprocal(rowscale[:, 1:2], rowscale[:, 0:1]))
                link(nc.vector.tensor_tensor(rowscale[:, 2:3], rowscale[:, 1:2], att[:, bass.ds(i, 1)], ALU.mult))
                dve.wait_ge(pv_done, C * (i + 1))
                dve.wait_ge(x_biased, i + 1)
                row = x1[:, bass.ds(i, 1), :].rearrange("p a d -> p (a d)")
                nc.vector.scalar_tensor_tensor(out=y[:, :], in0=O[b][:, 0:D], scalar=rowscale[:, 2:3], in1=row,
                                               op0=ALU.mult, op1=ALU.add).then_inc(o_read, 1)
                dve.wait_ge(o_read, i + 1)
                link(normalise(row))

            dve.wait_ge(sup_copied, NG)
            nc.vector.tensor_reduce(small[:, 0:1], logits[:, :], AX.X, ALU.max).then_inc(node_dve, 1)
            dve.wait_ge(node_pool, 1)
            nc.vector.tensor_scalar(small[:, 2:3], small[:, 1:2], -1.0, None, ALU.mult).then_inc(node_dve, 1)
            dve.wait_ge(node_pool, 2)
            link(nc.vector.reciprocal(small[:, 5:6], small[:, 4:5]))
            link(nc.vector.tensor_scalar(att[:, :], att[:, :], small[:, 5:6], None, ALU.mult))

            mask_and_max(0, 0)
            weigh(0, 0)

            def step(i, b):
                mask_and_max(i + 1, (b + 1) % 2)
                weigh(i + 1, (b + 1) % 2)
                finish_first(i, b)

            step(0, 0)
            before = links[0]
            step(1, 1)
            per_step = links[0] - before
            with dve.Fori(2, NB - 3, 2) as i0:
                for b in range(2):
                    links[0] = before + per_step * (i0 + b - 1)
                    step(i0 + b, b)
            links[0] = before + per_step * (NB - 3)
            step(NB - 2, 0)
            finish_first(NB - 1, 1)

            dve.wait_ge(deg_ready, 1)
            link(nc.vector.tensor_scalar(nv[:, :], E[0][:, 0:NB], 1.0, None, ALU.add))
            rsqrt(nv[:, :], ny[:, :], nt[:, :])
            link(nc.vector.tensor_scalar(nt[:, :], nv[:, :], 0.0, None, ALU.not_equal))
            link(nc.vector.tensor_tensor(dinv[:, :], ny[:, :], nt[:, :], ALU.mult))
            with dve.Fori(0, NB, 1) as j:
                nc.vector.tensor_scalar(sup[:, bass.ds(j, 1), :].rearrange("p a d -> p (a d)"),
                                        x1[:, bass.ds(j, 1), :].rearrange("p a d -> p (a d)"),
                                        dinv[:, bass.ds(j, 1)], None, ALU.mult).then_inc(g_ready, 1)
            dve.wait_ge(g_ready, NB)

            def scale_rows(j, b):
                dve.wait_ge(pv_done, C * (NB + 1) + C * j)
                dve.wait_ge(y_ready, j)
                g = sup[:, bass.ds(j, 1), :].rearrange("p a d -> p (a d)")
                nc.vector.tensor_tensor(y[:, :], O[b][:, 0:D], g, ALU.add).then_inc(o_read, 1)
                dve.wait_ge(o_read, NB + j + 1)
                nc.vector.tensor_scalar(hm[:, :], y[:, :], dinv[:, bass.ds(j, 1)], None, ALU.mult
                                        ).then_inc(hm_ready, 1)

            def bias_linear(j):
                dve.wait_ge(lin_ready, j + 1)
                nc.vector.tensor_tensor(th[:, :], E[1][:, 0:D], b1_sb[:, :], ALU.add).then_inc(lin_biased, 1)

            def finish_second(j, b, first=False):
                dve.wait_ge(tanh_done, j + 1)
                if not first:
                    dve.wait_ge(stored[b], 8 * (j - b))
                row = x1[:, bass.ds(j, 1), :].rearrange("p a d -> p (a d)")
                link(nc.vector.tensor_tensor(y[:, :], th[:, :], row, ALU.add))
                normalise(obuf[:, b, :]).then_inc(y_ready, 1)

            def tail(j, b, first=False):
                bias_linear(j)
                finish_second(j, b, first)

            scale_rows(0, 0)
            tail(0, 0, first=True)
            scale_rows(1, 1)
            before2 = links[0]
            tail(1, 1, first=True)
            per_tail = links[0] - before2
            with dve.Fori(2, NB - 1, 2) as j0:
                for b in range(2):
                    scale_rows(j0 + b, b)
                    links[0] = before2 + per_tail * (j0 + b - 1)
                    tail(j0 + b, b)


_INS = ['x', 'adj', 'L0_gnn_weight', 'L0_gnn_bias', 'L0_gnn_node_w', 'L0_gnn_edge_w', 'L1_gnn_W', 'L1_gnn_b']
_OUTS = [((4096, 256), 'float32')]


def kernel(**inputs):
    import numpy as _np
    import concourse.bacc as _bacc
    from concourse import mybir as _mybir
    from concourse.bass_utils import run_bass_kernel_spmd as _run

    nc = _bacc.Bacc("TRN2", target_bir_lowering=False, num_devices=1)
    arrays, args = {}, []
    for name in _INS:
        a = _np.ascontiguousarray(inputs[name])
        arrays[f"in_{name}_dram"] = a
        args.append(nc.dram_tensor(f"in_{name}_dram", a.shape, _mybir.dt.from_np(a.dtype), kind="ExternalInput").ap())
    for i, (shape, dtype) in enumerate(_OUTS):
        dt = _mybir.dt.from_np(_np.dtype(dtype))
        args.append(nc.dram_tensor(f"out_{i}_dram", shape, dt, kind="ExternalOutput").ap())
    general_path(nc, *args)
    r = _run(nc, [arrays], core_ids=[0])
    got = tuple(r.results[0][f"out_{i}_dram"] for i in range(len(_OUTS)))
    return got[0]
```

```python
from contextlib import ExitStack

import concourse.bass as bass
from concourse import mybir

P = 128
ALU = mybir.AluOpType
ACT = mybir.ActivationFunctionType
AX = mybir.AxisListType
F32 = mybir.dt.float32
I32 = mybir.dt.int32
F16 = mybir.dt.float16
BF16 = mybir.dt.bfloat16
RMAX = bass.bass_isa.ReduceOp.max
RADD = bass.bass_isa.ReduceOp.add

NEG_BIG = -9000000000000000.0
EPS = 1e-5
RSQRT_SEED = 0x5F3759DF
RSQRT_STEPS = 3


P_SCALE = 4096.0
G_SCALE = 2048.0


def rows(t, i):
    return t[:, bass.ds(i, 1), :].rearrange("p a d -> p (a d)")

def split_path(nc, flag, adj16, x, adj, w0, b0, node_w, edge_w, w1, b1, out):
    N, D = x.shape
    NB = N // P
    KD = D // P
    CH = 512
    C = N // CH
    TJ = CH // P
    HALF = N // 2
    HC = HALF // CH
    WC = 2 * CH
    W = N // WC
    TW = WC // P
    GR = CH // P
    NG = NB // GR

    with ExitStack() as ctx:
        def sb(name, shape, dt=F32):
            return ctx.enter_context(nc.sbuf_tensor("s_" + name, shape, dt))

        def psum(name, shape, dt=F32):
            return ctx.enter_context(nc.psum_tensor("s_" + name, shape, dt))

        def sem(name):
            return ctx.enter_context(nc.semaphore("s_" + name))

        hT = sb("hT", [P, 2, KD, N], F16)
        sup = sb("sup", [P, NB, 2 * D], F16)
        x1 = sb("x1", [P, NB, D])
        A = sb("A", [P, 2, HALF])
        A16 = sb("A16", [P, 2, N], F16)
        M = sb("M", [P, 2, N])
        colsum = sb("colsum", [P, N], F16)
        negs = sb("negs", [P, 2, CH], BF16)
        PH = sb("PH", [P, 4, CH], F16)
        PL = sb("PL", [P, 4, CH], F16)
        AT = [PH[:, 2 * i:2 * i + 2, :].rearrange("p a n -> p (a n)") for i in range(2)] + \
             [PL[:, 2 * i:2 * i + 2, :].rearrange("p a n -> p (a n)") for i in range(2)]
        hI = sb("hI", [P, 2, 2, KD, P], F16)
        edge_sb = sb("edge_sb", [P, KD, D])
        w0n = sb("w0n", [P, KD, D + 1])
        w1T = sb("w1T", [P, KD, D])
        b0_sb = sb("b0_sb", [P, D])
        b1_sb = sb("b1_sb", [P, D])
        ident = sb("ident", [P, P])
        ident16 = sb("ident16", [P, P], F16)
        ones = sb("ones", [P, P])
        ones16 = sb("ones16", [P, 2], F16)
        unequal = sb("unequal", [P, NB * C])
        chunk_junk = sb("chunk_junk", [P, CH], F16)
        h_guard = sb("h_guard", [P, NG])
        sup_guard = sb("sup_guard", [P, NB])
        guard = sb("guard", [P, 6])
        logits = sb("logits", [P, NB])
        att = sb("att", [P, NB])
        small = sb("small", [P, 8])
        chunkmax = sb("chunkmax", [P, C])
        negmax = sb("negmax", [P, 2])
        chunksum = sb("chunksum", [P, 2, C])
        rowscale = sb("rowscale", [P, 4])
        stats = sb("stats", [P, 6])
        meanvar = sb("meanvar", [P, 2])
        nv = sb("nv", [P, NB])
        ny = sb("ny", [P, NB])
        nt = sb("nt", [P, NB])
        dinv = sb("dinv", [P, NB])
        dscaled = sb("dscaled", [P, NB])
        dunscaled = sb("dunscaled", [P, NB])
        scratch = sb("scratch", [P, 1])
        y = sb("y", [P, D])
        y2 = sb("y2", [P, D])
        hm = sb("hm", [P, D])
        hmT = sb("hmT", [P, KD, P])
        th = sb("th", [P, D])
        obuf = sb("obuf", [P, 2, D])
        w1_sb = obuf
        b0_row, b1_row = y[0:1, :], hm[0:1, :]
        xg = [A[:, b, 0:GR * D].rearrange("p (r d) -> p r d", r=GR) for b in range(2)]
        xT = [M[:, b, 0:KD * CH].rearrange("p (k n) -> p k n", k=KD) for b in range(2)]

        E4 = psum("E4", [P, 4 * CH])
        E = [E4[:, i * CH:(i + 1) * CH] for i in range(4)]
        EA, EB = E4[:, 0:2 * CH], E4[:, 2 * CH:4 * CH]
        T2 = psum("T2", [P, 2 * CH])
        T = [T2[:, i * CH:(i + 1) * CH] for i in range(2)]
        T16 = [t.bitcast(F16) for t in T]
        O = [psum(f"O{i}", [P, CH]) for i in range(2)]
        S4 = T + [o[:, :] for o in O]

        w_loaded = sem("w_loaded")
        x1_loaded = sem("x1_loaded")
        xg_loaded = [sem(f"xg_loaded{i}") for i in range(2)]
        a_loaded = [sem(f"a_loaded{i}") for i in range(2)]
        a16_stored = [sem(f"a16_stored{i}") for i in range(2)]
        a16_loaded = [sem(f"a16_loaded{i}") for i in range(2)]
        ident_zero = sem("ident_zero")
        consts = sem("consts")
        bias_ready = sem("bias_ready")
        bias_copied = sem("bias_copied")
        wt_ready = sem("wt_ready")
        wt_copied = sem("wt_copied")
        xt_ready = sem("xt_ready")
        xt_copied_act = sem("xt_copied_act")
        xt_copied_dve = sem("xt_copied_dve")
        h_ready = sem("h_ready")
        h_high = sem("h_high")
        h_split = sem("h_split")
        sup_ready = sem("sup_ready")
        sup_high = sem("sup_high")
        sup_split = sem("sup_split")
        node_dve = sem("node_dve")
        node_pool = sem("node_pool")
        node_act = sem("node_act")
        hi_staged = sem("hi_staged")
        x_biased = sem("x_biased")
        a16_ready = sem("a16_ready")
        a_checked = sem("a_checked")
        a16_summed = sem("a16_summed")
        negs_ready = sem("negs_ready")
        e_ready = sem("e_ready")
        e_masked = sem("e_masked")
        negmax_ready = sem("negmax_ready")
        p_ready = sem("p_ready")
        t_ready = sem("t_ready")
        t_high = sem("t_high")
        t_split = sem("t_split")
        pv_done = sem("pv_done")
        o_read = sem("o_read")
        row_done = sem("row_done")
        deg_ready = sem("deg_ready")
        d_ready = sem("d_ready")
        g_high = sem("g_high")
        g_split = sem("g_split")
        at_ready = sem("at_ready")
        at_copied = sem("at_copied")
        ag_done = sem("ag_done")
        o2_read = sem("o2_read")
        hm_ready = sem("hm_ready")
        hmt_ready = sem("hmt_ready")
        hmt_copied = sem("hmt_copied")
        lin_ready = sem("lin_ready")
        lin_biased = sem("lin_biased")
        tanh_done = sem("tanh_done")
        y_ready = sem("y_ready")
        stored = [sem(f"stored{i}") for i in range(2)]
        bad_rows = sem("bad_rows")
        bad_all = sem("bad_all")
        flag_ready = sem("flag_ready")
        dve_chain = sem("dve_chain")

        x_groups = x.rearrange("(g r p) d -> g p r d", p=P, r=GR)
        x_rows = x.rearrange("(b p) d -> p b d", p=P)
        adj_halves = adj.rearrange("(b p) (h n) -> b h p n", p=P, h=2)
        adj16_rows = adj16.rearrange("(b p) n -> b p n", p=P)
        out_rows = out.rearrange("(b p) d -> b p d", p=P)

        block = ctx.enter_context(nc.Block())

        @block.sync
        def _(sp):
            sp.dma_start(edge_sb[:, :, :], edge_w.rearrange("(k p) d -> p k d", p=P)).then_inc(w_loaded, 16)
            sp.dma_start(w0n[:, :, 0:D], w0.rearrange("(k p) d -> p k d", p=P)).then_inc(w_loaded, 16)
            sp.dma_start(w0n[:, :, D:D + 1], node_w.rearrange("(k p) d -> p k d", p=P),
                         allow_slow_non_contiguous=True).then_inc(w_loaded, 16)
            sp.dma_start(w1_sb[:, :, :], w1.rearrange("(k p) d -> p k d", p=P)).then_inc(w_loaded, 16)
            sp.dma_start(b0_row[:, :], b0.rearrange("(a d) -> a d", a=1)).then_inc(w_loaded, 16)
            sp.dma_start(b1_row[:, :], b1.rearrange("(a d) -> a d", a=1)).then_inc(w_loaded, 16)
            for g in range(2):
                sp.dma_start(xg[g], x_groups[g]).then_inc(xg_loaded[g], 16)
            with sp.Fori(2, NG - 1, 2) as g0:
                for b in range(2):
                    g = g0 + b
                    sp.wait_ge(xt_ready, g - 1)
                    sp.dma_start(xg[b], x_groups[bass.ds(g, 1)].rearrange("a p r d -> (a p) r d")
                                 ).then_inc(xg_loaded[b], 16)
            sp.dma_start(x1[:, :, :], x_rows).then_inc(x1_loaded, 16)
            sp.wait_ge(xt_ready, NG)
            for h in range(2):
                sp.dma_start(A[:, h, :], adj_halves[0, h]).then_inc(a_loaded[h], 16)
            for h in range(2):
                sp.wait_ge(a_checked, HC * (h + 1))
                sp.dma_start(A[:, h, :], adj_halves[1, h]).then_inc(a_loaded[h], 16)
            with sp.Fori(0, NB - 3, 2) as i0:
                for b in range(2):
                    i = i0 + b
                    for h in range(2):
                        sp.wait_ge(a_checked, C * (i + 1) + HC * (h + 1))
                        sp.dma_start(A[:, h, :], adj_halves[bass.ds(i + 2, 1), h].rearrange("a p n -> (a p) n")
                                     ).then_inc(a_loaded[h], 16)
                    sp.wait_ge(a16_ready, C * (i + 1))
                    sp.dma_start(adj16_rows[bass.ds(i, 1)].rearrange("a p n -> (a p) n"), A16[:, b, :]
                                 ).then_inc(a16_stored[b], 16)
            for b in range(2):
                sp.wait_ge(a16_ready, C * (NB - 1 + b))
                sp.dma_start(adj16_rows[NB - 2 + b], A16[:, b, :]).then_inc(a16_stored[b], 16)
            for b in range(2):
                sp.wait_ge(a16_stored[b], 8 * NB)
                sp.wait_ge(negs_ready, C * NB)
                sp.wait_ge(a16_summed, NB)
            for b in range(2):
                sp.dma_start(A16[:, b, :], adj16_rows[b]).then_inc(a16_loaded[b], 16)
            with sp.Fori(0, NB - 3, 2) as j0:
                for b in range(2):
                    j = j0 + b
                    sp.wait_ge(at_ready, W * (j + 1))
                    sp.dma_start(A16[:, b, :], adj16_rows[bass.ds(j + 2, 1)].rearrange("a p n -> (a p) n")
                                 ).then_inc(a16_loaded[b], 16)
                    sp.wait_ge(y_ready, j + 1)
                    sp.dma_start(out_rows[bass.ds(j, 1)].rearrange("a p d -> (a p) d"), obuf[:, b, :]
                                 ).then_inc(stored[b], 16)
            for b in range(2):
                sp.wait_ge(y_ready, NB - 1 + b)
                sp.dma_start(out_rows[NB - 2 + b], obuf[:, b, :]).then_inc(stored[b], 16)
            for b in range(2):
                sp.wait_ge(stored[b], 16 * (NB // 2))

        @block.tensor
        def _(pe):
            pe.wait_ge(consts, 6)
            pe.wait_ge(w_loaded, 96)
            nc.tensor.matmul(O[0][:, 0:D], ones[0:1, :], b0_row[:, :], start=True, stop=True)
            nc.tensor.matmul(O[1][:, 0:D], ones[0:1, :], b1_row[:, :], start=True, stop=True
                             ).then_inc(bias_ready, 1)
            for k in range(KD):
                for o in range(KD):
                    last = nc.tensor.transpose(T[0][:, (k * KD + o) * P:(k * KD + o + 1) * P],
                                               w1_sb[:, o, k * P:(k + 1) * P], ident[:, :])
            last.then_inc(wt_ready, 1)

            def transpose_group(g, b):
                pe.wait_ge(xg_loaded[b], 8 * (g - b) + 16)
                for k in range(KD):
                    for r in range(GR):
                        last = nc.tensor.transpose(EA[:, k * CH + r * P:k * CH + (r + 1) * P],
                                                   xg[b][:, r, k * P:(k + 1) * P], ident[:, :])
                last.then_inc(xt_ready, 1)

            def project_group(g, b, first=False):
                pe.wait_ge(xt_copied_act, g + 1)
                pe.wait_ge(xt_copied_dve, g + 1)
                if not first:
                    pe.wait_ge(h_split, g)
                for m in range(KD):
                    for k in range(KD):
                        last = nc.tensor.matmul(EB[:, m * CH:(m + 1) * CH], edge_sb[:, k, m * P:(m + 1) * P],
                                                xT[b][:, k, :], start=(k == 0), stop=(k == KD - 1))
                last.then_inc(h_ready, 1)
                if not first:
                    pe.wait_ge(sup_split, g)
                for r in range(GR):
                    for k in range(KD):
                        last = nc.tensor.matmul(S4[r][:, 0:D + 1], xT[b][:, k, r * P:(r + 1) * P], w0n[:, k, :],
                                                start=(k == 0), stop=(k == KD - 1))
                last.then_inc(sup_ready, 1)

            def next_transpose(g, b):
                pe.wait_ge(xt_copied_act, g)
                pe.wait_ge(xt_copied_dve, g)
                transpose_group(g, b)

            transpose_group(0, 0)
            pe.wait_ge(bias_copied, 1)
            pe.wait_ge(wt_copied, 1)
            next_transpose(1, 1)
            project_group(0, 0, first=True)
            next_transpose(2, 0)
            project_group(1, 1)
            with pe.Fori(2, NG - 3, 2) as g0:
                for b in range(2):
                    next_transpose(g0 + b + 1, (b + 1) % 2)
                    project_group(g0 + b, b)
            next_transpose(NG - 1, 1)
            project_group(NG - 2, 0)
            project_group(NG - 1, 1)

            def scores(i, b, first=False):
                pe.wait_ge(hi_staged, i + 1)
                for c in range(C):
                    if not (first and c < 4):
                        pe.wait_ge(e_masked, C * i + c - 3)
                    terms = [(k, s, m) for k in range(KD) for s, m in ((0, 0), (0, 1), (1, 0))]
                    for n, (k, s, m) in enumerate(terms):
                        last = nc.tensor.matmul(E[c % 4], hI[:, b, s, k, :], hT[:, m, k, c * CH:(c + 1) * CH],
                                                start=(n == 0), stop=(n == len(terms) - 1))
                    last.then_inc(e_ready, 1)

            def transpose_chunk(i, b, c, first=False):
                pe.wait_ge(p_ready, C * i + c + 1)
                if not (first and c < 2):
                    pe.wait_ge(t_split, C * i + c - 1)
                for t in range(TJ):
                    col = c * CH + t * P
                    last = nc.tensor.transpose(T[c % 2][:, t * P:(t + 1) * P], M[:, b, col:col + P], ident[:, :])
                last.then_inc(t_ready, 1)

            def product_chunk(i, b, c):
                pe.wait_ge(t_high, C * i + c + 1)
                pe.wait_ge(t_split, C * i + c + 1)
                for t in range(TJ):
                    j = c * TJ + t
                    nc.tensor.matmul(O[b][:, :], PH[:, c % 4, t * P:(t + 1) * P], sup[:, j, :],
                                     start=(j == 0), stop=False)
                    last = nc.tensor.matmul(O[b][:, 0:D], PL[:, c % 4, t * P:(t + 1) * P], sup[:, j, 0:D],
                                            start=False, stop=(j == NB - 1))
                last.then_inc(pv_done, 1)

            def attend(i, b, first=False):
                for c in range(C):
                    transpose_chunk(i, b, c, first)
                    if c == 1 and not first:
                        pe.wait_ge(o_read, i - 1)
                    if c > 0:
                        product_chunk(i, b, c - 1)
                product_chunk(i, b, C - 1)

            pe.wait_ge(h_split, NG)
            pe.wait_ge(sup_split, NG)
            scores(0, 0, first=True)
            scores(1, 1)
            attend(0, 0, first=True)
            scores(2, 0)
            attend(1, 1)
            with pe.Fori(2, NB - 3, 2) as i0:
                for b in range(2):
                    scores(i0 + b + 1, (b + 1) % 2)
                    attend(i0 + b, b)
            scores(NB - 1, 1)
            attend(NB - 2, 0)
            attend(NB - 1, 1)

            pe.wait_ge(a16_summed, NB)
            for t in range(NB):
                last = nc.tensor.matmul(E4[:, t:t + 1], colsum[:, t * P:(t + 1) * P], ones16[:, 0:1],
                                        start=True, stop=True)
            last.then_inc(deg_ready, 1)

            def transpose_adj(j, b, w, first=False):
                if w == 0:
                    pe.wait_ge(a16_loaded[b], 8 * (j - b) + 16)
                if not (first and w < 2):
                    pe.wait_ge(at_copied, W * j + w - 1)
                for t in range(TW):
                    col = w * WC + t * P
                    last = nc.tensor.transpose(T16[w % 2][:, t * P:(t + 1) * P], A16[:, b, col:col + P],
                                               ident16[:, :])
                last.then_inc(at_ready, 1)

            def aggregate_chunk(j, b, w, first=False):
                pe.wait_ge(at_copied, W * j + w + 1)
                if first:
                    pe.wait_ge(g_split, TW * (w + 1))
                for t in range(TW):
                    jj = w * TW + t
                    last = nc.tensor.matmul(O[b][:, :], AT[w % 4][:, t * P:(t + 1) * P], sup[:, jj, :],
                                            start=(jj == 0), stop=(jj == NB - 1))
                last.then_inc(ag_done, 1)

            def hm_transpose(j):
                pe.wait_ge(hm_ready, j + 1)
                for k in range(KD):
                    last = nc.tensor.transpose(E[0][:, k * P:(k + 1) * P], hm[:, k * P:(k + 1) * P], ident[:, :])
                last.then_inc(hmt_ready, 1)

            def hm_linear(j, first=False):
                pe.wait_ge(hmt_copied, j + 1)
                if not first:
                    pe.wait_ge(lin_biased, j)
                for k in range(KD):
                    last = nc.tensor.matmul(E[1][:, 0:D], hmT[:, k, :], w1T[:, k, :],
                                            start=(k == 0), stop=(k == KD - 1))
                last.then_inc(lin_ready, 1)

            def aggregate(j, b, first=False, second=False):
                for w in range(W):
                    transpose_adj(j, b, w, first)
                    if w == 1 and not (first or second):
                        pe.wait_ge(o2_read, j - 1)
                    if w > 0:
                        aggregate_chunk(j, b, w - 1, first)
                    if w == 2 and not first:
                        hm_transpose(j - 1)
                    if w == 3 and not first:
                        hm_linear(j - 1, first=second)
                aggregate_chunk(j, b, W - 1, first)

            pe.wait_ge(t_split, C * NB)
            pe.wait_ge(o_read, NB)
            aggregate(0, 0, first=True)
            aggregate(1, 1, second=True)
            with pe.Fori(2, NB - 1, 2) as j0:
                for b in range(2):
                    aggregate(j0 + b, b)
            hm_transpose(NB - 1)
            hm_linear(NB - 1)

        @block.gpsimd
        def _(pool):
            nc.gpsimd.memset(ident[:, :], 0.0).then_inc(ident_zero, 1)
            nc.gpsimd.memset(ident16[:, :], 0.0).then_inc(ident_zero, 1)
            nc.gpsimd.memset(ones[:, :], 1.0).then_inc(consts, 1)
            nc.gpsimd.memset(ones16[:, :], 1.0).then_inc(consts, 1)
            pool.wait_ge(ident_zero, 2)
            for m in (ident, ident16):
                nc.gpsimd.affine_select(out=m[:, :], in_=m[:, :], compare_op=ALU.not_equal, fill=1.0, base=0,
                                        pattern=[[-1, P]], channel_multiplier=1).then_inc(consts, 1)
            nc.gpsimd.memset(colsum[:, :], 0.0).then_inc(consts, 1)
            nc.gpsimd.memset(guard[:, :], 0.0).then_inc(consts, 1)
            pool.wait_ge(bias_copied, 1)
            pool.wait_ge(x1_loaded, 16)
            pool.wait_ge(h_split, NG)

            def stage(i, b):
                for s in range(2):
                    last = nc.gpsimd.tensor_copy(hI[:, b, s, :, :], hT[:, s, :, bass.ds(i * P, P)])
                last.then_inc(hi_staged, 1)

            def add_bias(i):
                nc.gpsimd.tensor_tensor(rows(x1, i), rows(x1, i), b0_sb[:, :], ALU.add).then_inc(x_biased, 1)

            def add_columns(i, b, first=False):
                pool.wait_ge(a16_ready, C * (i + 1))
                if not first:
                    pool.wait_ge(a16_summed, i)
                nc.gpsimd.tensor_tensor(colsum[:, :], colsum[:, :], A16[:, b, :], ALU.add).then_inc(a16_summed, 1)

            stage(0, 0)
            stage(1, 1)
            pool.wait_ge(node_dve, 1)
            nc.gpsimd.partition_all_reduce(small[:, 1:2], small[:, 0:1], P, RMAX).then_inc(node_pool, 1)
            pool.wait_ge(node_act, 1)
            nc.gpsimd.partition_all_reduce(small[:, 4:5], small[:, 3:4], P, RADD).then_inc(node_pool, 1)
            pool.wait_ge(consts, 6)
            add_bias(0)
            add_columns(0, 0, first=True)
            add_bias(1)
            add_columns(1, 1)
            with pool.Fori(2, NB - 1, 2) as i0:
                for b in range(2):
                    i = i0 + b
                    pool.wait_ge(e_ready, C * (i - 1))
                    stage(i, b)
                    add_bias(i)
                    add_columns(i, b)
            pool.wait_ge(bad_rows, 1)
            nc.gpsimd.partition_all_reduce(guard[:, 5:6], guard[:, 4:5], P, RMAX).then_inc(bad_all, 1)

        @block.scalar
        def _(act):
            act.wait_ge(bias_ready, 1)
            nc.scalar.copy(b0_sb[:, :], O[0][:, 0:D])
            nc.scalar.copy(b1_sb[:, :], O[1][:, 0:D]).then_inc(bias_copied, 1)
            act.wait_ge(wt_ready, 1)
            nc.scalar.copy(w1T[:, :, :], T[0].rearrange("p (k n) -> p k n", k=KD)).then_inc(wt_copied, 1)

            def copy_group(g, b, first=False):
                act.wait_ge(xt_ready, g + 1)
                if not first:
                    act.wait_ge(sup_ready, g - 1)
                nc.scalar.copy(xT[b][:, 0, :], EA[:, 0:CH]).then_inc(xt_copied_act, 1)

            def high_parts(g):
                act.wait_ge(h_ready, g + 1)
                nc.scalar.copy(hT[:, 0, :, bass.ds(g * CH, CH)], EB.rearrange("p (k n) -> p k n", k=KD)
                               ).then_inc(h_high, 1)
                act.wait_ge(sup_ready, g + 1)
                for r in range(GR):
                    last = nc.scalar.copy(rows(sup, g * GR + r)[:, 0:D], S4[r][:, 0:D])
                last.then_inc(sup_high, 1)

            copy_group(0, 0, first=True)
            copy_group(1, 1, first=True)
            with act.Fori(0, NG - 3, 2) as g0:
                for b in range(2):
                    high_parts(g0 + b)
                    copy_group(g0 + b + 2, b)
            high_parts(NG - 2)
            high_parts(NG - 1)
            act.wait_ge(node_dve, 2)
            nc.scalar.activation(att[:, :], logits[:, :], ACT.Exp, bias=small[:, 2:3], scale=1.0,
                                 accum_out=small[:, 3:4]).then_inc(node_act, 1)

            def exps(i, b, c):
                if c == 0:
                    act.wait_ge(negmax_ready, i + 1)
                nc.scalar.activation(M[:, b, c * CH:(c + 1) * CH], M[:, b, c * CH:(c + 1) * CH], ACT.Exp,
                                     bias=negmax[:, b:b + 1], scale=1.0,
                                     accum_out=chunksum[:, b, c:c + 1]).then_inc(p_ready, 1)

            def high_transposed(i, c, first=False):
                act.wait_ge(t_ready, C * i + c + 1)
                if not (first and c < 4):
                    act.wait_ge(pv_done, C * i + c - 3)
                nc.scalar.activation(PH[:, c % 4, :], T[c % 2], ACT.Copy, scale=P_SCALE).then_inc(t_high, 1)

            def attend(i, b, first=False, last=False):
                for c in range(C):
                    high_transposed(i, c, first)
                    if not last:
                        exps(i + 1, (b + 1) % 2, c)

            for c in range(C):
                exps(0, 0, c)
            attend(0, 0, first=True)
            attend(1, 1)
            with act.Fori(2, NB - 3, 2) as i0:
                for b in range(2):
                    attend(i0 + b, b)
            attend(NB - 2, 0)
            attend(NB - 1, 1, last=True)

            act.wait_ge(d_ready, 1)
            act.wait_ge(row_done, NB)
            with act.Fori(0, NB, 1) as j:
                nc.scalar.activation(rows(sup, j)[:, 0:D], rows(x1, j), ACT.Copy, scale=dscaled[:, bass.ds(j, 1)]
                                     ).then_inc(g_high, 1)

            def copy_adj(j, w, first=False):
                act.wait_ge(at_ready, W * j + w + 1)
                if not first:
                    act.wait_ge(ag_done, W * j + w - 3)
                nc.scalar.copy(AT[w % 4], T16[w % 2]).then_inc(at_copied, 1)

            def copy_hmT(j):
                act.wait_ge(hmt_ready, j + 1)
                nc.scalar.copy(hmT[:, :, :], E[0][:, 0:D].rearrange("p (k n) -> p k n", k=KD)
                               ).then_inc(hmt_copied, 1)

            def tanh(j):
                act.wait_ge(lin_biased, j + 1)
                nc.scalar.activation(th[:, :], th[:, :], ACT.Tanh).then_inc(tanh_done, 1)

            def aggregate(j, first=False):
                for w in range(W):
                    copy_adj(j, w, first)
                    if w == 2 and not first:
                        copy_hmT(j - 1)
                if not first:
                    tanh(j - 1)

            aggregate(0, first=True)
            with act.Fori(1, NB, 1) as j:
                aggregate(j)
            copy_hmT(NB - 1)
            tanh(NB - 1)

        @block.vector
        def _(dve):
            links = [0]

            def link(ins):
                links[0] = links[0] + 1
                ins.then_inc(dve_chain, 1)
                dve.wait_ge(dve_chain, links[0])

            def carry_wait():
                nc.vector.memset(scratch[:, :], 0.0)

            def rsqrt(v, r, t):
                link(nc.vector.tensor_scalar(r.bitcast(I32), v.bitcast(I32), -0.5, float(RSQRT_SEED),
                                             ALU.mult, ALU.add))
                for _ in range(RSQRT_STEPS):
                    link(nc.vector.scalar_tensor_tensor(out=t, in0=r, scalar=-0.5, in1=r, op0=ALU.mult,
                                                        op1=ALU.mult))
                    link(nc.vector.tensor_tensor(t, t, v, ALU.mult))
                    link(nc.vector.scalar_tensor_tensor(out=r, in0=t, scalar=1.5, in1=r, op0=ALU.add,
                                                        op1=ALU.mult))

            def copy_group(g, b, first=False):
                dve.wait_ge(xt_ready, g + 1)
                if not first:
                    dve.wait_ge(sup_ready, g - 1)
                nc.vector.tensor_copy(xT[b][:, 1, :], EA[:, CH:2 * CH]).then_inc(xt_copied_dve, 1)

            def low_parts(g):
                dve.wait_ge(h_high, g + 1)
                nc.vector.scalar_tensor_tensor(
                    out=hT[:, 1, :, bass.ds(g * CH, CH)], in0=EB.rearrange("p (k n) -> p k n", k=KD), scalar=1.0,
                    in1=hT[:, 0, :, bass.ds(g * CH, CH)], op0=ALU.mult, op1=ALU.subtract,
                    accum_out=h_guard[:, bass.ds(g, 1)]).then_inc(h_split, 1)
                dve.wait_ge(sup_high, g + 1)
                for r in range(GR):
                    j = g * GR + r
                    nc.vector.scalar_tensor_tensor(
                        out=rows(sup, j)[:, D:2 * D], in0=S4[r][:, 0:D], scalar=1.0, in1=rows(sup, j)[:, 0:D],
                        op0=ALU.mult, op1=ALU.subtract, accum_out=sup_guard[:, bass.ds(j, 1)])
                    last = nc.vector.tensor_copy(logits[:, bass.ds(j, 1)], S4[r][:, D:D + 1])
                last.then_inc(sup_split, 1)

            copy_group(0, 0, first=True)
            copy_group(1, 1, first=True)
            with dve.Fori(0, NG - 3, 2) as g0:
                for b in range(2):
                    low_parts(g0 + b)
                    copy_group(g0 + b + 2, b)
            low_parts(NG - 2)
            low_parts(NG - 1)

            dve.wait_ge(sup_split, NG)
            nc.vector.tensor_reduce(small[:, 0:1], logits[:, :], AX.X, ALU.max).then_inc(node_dve, 1)
            dve.wait_ge(node_pool, 1)
            nc.vector.tensor_scalar(small[:, 2:3], small[:, 1:2], -1.0, None, ALU.mult).then_inc(node_dve, 1)

            def zeros_and_ones(i, b, c):
                h = c // HC
                col = (c % HC) * CH
                if c % HC == 0:
                    dve.wait_ge(a_loaded[h], 16 * (i + 1))
                a, a16 = A[:, h, col:col + CH], A16[:, b, c * CH:(c + 1) * CH]
                nc.vector.tensor_scalar(a16, a, 0.0, None, ALU.is_gt).then_inc(a16_ready, 1)
                dve.wait_ge(a16_ready, C * i + c + 1)
                nc.vector.scalar_tensor_tensor(out=chunk_junk[:, :], in0=a, scalar=1.0, in1=a16, op0=ALU.mult,
                                               op1=ALU.not_equal, accum_out=unequal[:, bass.ds(i * C + c, 1)]
                                               ).then_inc(a_checked, 1)

            def free_a16(i, b):
                dve.wait_ge(a16_stored[b], 8 * (i - b))
                dve.wait_ge(a16_summed, i - 1)

            def mask_and_max(i, b, first=False):
                def mask(c):
                    nc.vector.tensor_scalar(negs[:, c % 2, :], A16[:, b, c * CH:(c + 1) * CH], 1.0, -NEG_BIG,
                                            ALU.subtract, ALU.mult).then_inc(negs_ready, 1)

                if not first:
                    dve.wait_ge(e_masked, C * i)
                dve.wait_ge(a16_ready, C * (i + 1))
                mask(0)
                for c in range(C):
                    dve.wait_ge(negs_ready, C * i + c + 1)
                    dve.wait_ge(e_ready, C * i + c + 1)
                    if not (first and c == 0):
                        dve.wait_ge(e_masked, C * i + c)
                    if c + 1 < C:
                        mask(c + 1)
                    else:
                        carry_wait()
                    nc.vector.tensor_tensor_reduce(
                        out=M[:, b, c * CH:(c + 1) * CH], in0=E[c % 4], in1=negs[:, c % 2, :], scale=1.0,
                        scalar=-3.0e38, op0=ALU.add, op1=ALU.max, accum_out=chunkmax[:, c:c + 1]
                    ).then_inc(e_masked, 1)
                dve.wait_ge(e_masked, C * i + C)
                nc.vector.tensor_reduce(negmax[:, b:b + 1], chunkmax[:, :], AX.X, ALU.max, negate=True
                                        ).then_inc(negmax_ready, 1)

            def low_transposed(i, c, first=False):
                dve.wait_ge(t_high, C * i + c + 1)
                if not (first and c < 4):
                    dve.wait_ge(pv_done, C * i + c - 3)
                nc.vector.scalar_tensor_tensor(out=PL[:, c % 4, :], in0=T[c % 2], scalar=P_SCALE,
                                               in1=PH[:, c % 4, :], op0=ALU.mult, op1=ALU.subtract
                                               ).then_inc(t_split, 1)

            def normalise(dst):
                link(nc.vector.bn_stats(stats[:, :], y[:, :]))
                carry_wait()
                link(nc.vector.bn_aggr(meanvar[:, :], stats[:, :]))
                link(nc.vector.tensor_scalar(nv[:, 0:1], meanvar[:, 1:2], EPS, None, ALU.add))
                rsqrt(nv[:, 0:1], ny[:, 0:1], nt[:, 0:1])
                return nc.vector.tensor_scalar(dst, y[:, :], meanvar[:, 0:1], ny[:, 0:1], ALU.subtract, ALU.mult)

            def finish_first(i, b, first=False):
                if not first:
                    dve.wait_ge(row_done, i)
                link(nc.vector.tensor_reduce(rowscale[:, 0:1], chunksum[:, b, :], AX.X, ALU.add))
                link(nc.vector.tensor_scalar(rowscale[:, 3:4], negmax[:, b:b + 1], -0.5 * NEG_BIG, 1.0 / P_SCALE,
                                             ALU.is_lt, ALU.mult))
                link(nc.vector.reciprocal(rowscale[:, 1:2], rowscale[:, 0:1]))
                link(nc.vector.scalar_tensor_tensor(out=rowscale[:, 2:3], in0=rowscale[:, 1:2],
                                                    scalar=rowscale[:, 3:4], in1=att[:, bass.ds(i, 1)],
                                                    op0=ALU.mult, op1=ALU.mult))
                dve.wait_ge(pv_done, C * (i + 1))
                dve.wait_ge(x_biased, i + 1)
                link(nc.vector.scalar_tensor_tensor(out=y2[:, :], in0=O[b][:, D:2 * D], scalar=rowscale[:, 2:3],
                                                    in1=rows(x1, i), op0=ALU.mult, op1=ALU.add))
                nc.vector.scalar_tensor_tensor(out=y[:, :], in0=O[b][:, 0:D], scalar=rowscale[:, 2:3],
                                               in1=y2[:, :], op0=ALU.mult, op1=ALU.add).then_inc(o_read, 1)
                dve.wait_ge(o_read, i + 1)
                normalise(rows(x1, i)).then_inc(row_done, 1)

            for c in range(C):
                zeros_and_ones(0, 0, c)
            for c in range(C):
                zeros_and_ones(1, 1, c)
            mask_and_max(0, 0, first=True)
            dve.wait_ge(node_pool, 2)
            link(nc.vector.reciprocal(small[:, 5:6], small[:, 4:5]))
            link(nc.vector.tensor_scalar(att[:, :], att[:, :], small[:, 5:6], None, ALU.mult))

            def step(i, b, first=False, ahead=True):
                mask_and_max(i + 1, (b + 1) % 2)
                if ahead:
                    free_a16(i + 2, b)
                for c in range(C):
                    low_transposed(i, c, first)
                    if ahead:
                        zeros_and_ones(i + 2, b, c)
                finish_first(i, b, first)

            step(0, 0, first=True)
            before = links[0]
            step(1, 1)
            per_step = links[0] - before
            with dve.Fori(2, NB - 3, 2) as i0:
                for b in range(2):
                    links[0] = before + per_step * (i0 + b - 1)
                    step(i0 + b, b)
            links[0] = before + per_step * (NB - 3)
            step(NB - 2, 0, ahead=False)
            for c in range(C):
                low_transposed(NB - 1, c)
            finish_first(NB - 1, 1)

            dve.wait_ge(row_done, NB)
            dve.wait_ge(deg_ready, 1)
            link(nc.vector.tensor_scalar(nv[:, :], E4[:, 0:NB], 1.0, None, ALU.add))
            rsqrt(nv[:, :], dinv[:, :], nt[:, :])
            nc.vector.tensor_scalar(dscaled[:, :], dinv[:, :], G_SCALE, None, ALU.mult).then_inc(d_ready, 1)
            link(nc.vector.tensor_scalar(dunscaled[:, :], dinv[:, :], 1.0 / G_SCALE, None, ALU.mult))
            with dve.Fori(0, NB, 1) as j:
                dve.wait_ge(g_high, j + 1)
                nc.vector.scalar_tensor_tensor(out=rows(sup, j)[:, D:2 * D], in0=rows(x1, j),
                                               scalar=dscaled[:, bass.ds(j, 1)], in1=rows(sup, j)[:, 0:D],
                                               op0=ALU.mult, op1=ALU.subtract).then_inc(g_split, 1)

            dve.wait_ge(a_checked, C * NB)
            link(nc.vector.tensor_reduce(guard[:, 0:1], unequal[:, :], AX.X, ALU.max))
            link(nc.vector.tensor_reduce(guard[:, 1:2], h_guard[:, :], AX.X, ALU.add))
            link(nc.vector.tensor_reduce(guard[:, 2:3], sup_guard[:, :], AX.X, ALU.add))
            link(nc.vector.tensor_tensor(guard[:, 3:4], guard[:, 1:2], guard[:, 2:3], ALU.add))
            link(nc.vector.tensor_scalar(guard[:, 3:4], guard[:, 3:4], 0.0, 0.0, ALU.mult, ALU.is_equal))
            link(nc.vector.tensor_scalar(guard[:, 0:1], guard[:, 0:1], 0.0, 1.0, ALU.is_gt, ALU.add))
            nc.vector.tensor_tensor(guard[:, 4:5], guard[:, 0:1], guard[:, 3:4], ALU.subtract).then_inc(bad_rows, 1)

            def scale_rows(j, b, first=False):
                dve.wait_ge(ag_done, W * (j + 1))
                if not first:
                    dve.wait_ge(y_ready, j)
                link(nc.vector.scalar_tensor_tensor(out=y2[:, :], in0=rows(x1, j),
                                                    scalar=dscaled[:, bass.ds(j, 1)], in1=O[b][:, 0:D],
                                                    op0=ALU.mult, op1=ALU.add))
                nc.vector.tensor_tensor(y[:, :], y2[:, :], O[b][:, D:2 * D], ALU.add).then_inc(o2_read, 1)
                dve.wait_ge(o2_read, j + 1)
                nc.vector.tensor_scalar(hm[:, :], y[:, :], dunscaled[:, bass.ds(j, 1)], None, ALU.mult
                                        ).then_inc(hm_ready, 1)

            def tail(j, b, first=False):
                dve.wait_ge(lin_ready, j + 1)
                nc.vector.tensor_tensor(th[:, :], E[1][:, 0:D], b1_sb[:, :], ALU.add).then_inc(lin_biased, 1)
                dve.wait_ge(tanh_done, j + 1)
                if not first:
                    dve.wait_ge(stored[b], 8 * (j - b))
                link(nc.vector.tensor_tensor(y[:, :], th[:, :], rows(x1, j), ALU.add))
                normalise(obuf[:, b, :]).then_inc(y_ready, 1)

            before2 = links[0]
            scale_rows(0, 0, first=True)
            tail(0, 0, first=True)
            scale_rows(1, 1)
            tail(1, 1, first=True)
            per_block = (links[0] - before2) // 2
            with dve.Fori(2, NB - 1, 2) as j0:
                for b in range(2):
                    links[0] = before2 + per_block * (j0 + b)
                    scale_rows(j0 + b, b)
                    tail(j0 + b, b)

            dve.wait_ge(bad_all, 1)
            nc.vector.tensor_copy(flag[:, :], guard[:, 5:6]).then_inc(flag_ready, 1)
            dve.wait_ge(flag_ready, 1)


def general_path(nc, flag, x, adj, w0, b0, node_w, edge_w, w1, b1, out):
    N, D = x.shape
    NB = N // P
    KD = D // P
    CH = 512
    UN = CH
    U = N // UN
    C = N // CH
    TJ = CH // P
    GR = CH // P
    NG = NB // GR

    with ExitStack() as ctx:
        def sb(name, shape, dt=F32):
            return ctx.enter_context(nc.sbuf_tensor(name, shape, dt))

        def psum(name, shape, dt=F32):
            return ctx.enter_context(nc.psum_tensor(name, shape, dt))

        def sem(name):
            return ctx.enter_context(nc.semaphore(name))

        hT = sb("hT", [P, KD, N])
        sup = sb("sup", [P, NB, D])
        x1 = sb("x1", [P, NB, D])
        A = sb("A", [P, 2, N])
        M = sb("M", [P, 2, N])
        colsum = sb("colsum", [P, N])
        negs = sb("negs", [P, 2, CH])
        PT = sb("PT", [P, 4, CH])
        hI = sb("hI", [P, 2, KD, P])
        edge_sb = sb("edge_sb", [P, KD, D])
        w0n = sb("w0n", [P, KD, D + 1])
        w1T = sb("w1T", [P, KD, D])
        b0_sb = sb("b0_sb", [P, D])
        b1_sb = sb("b1_sb", [P, D])
        ident = sb("ident", [P, P])
        ones = sb("ones", [P, P])
        logits = sb("logits", [P, NB])
        att = sb("att", [P, NB])
        small = sb("small", [P, 8])
        unitmax = sb("unitmax", [P, U])
        negmax = sb("negmax", [P, 2])
        unitsum = sb("unitsum", [P, 2, U])
        rowscale = sb("rowscale", [P, 4])
        stats = sb("stats", [P, 6])
        meanvar = sb("meanvar", [P, 2])
        nv = sb("nv", [P, NB])
        ny = sb("ny", [P, NB])
        nt = sb("nt", [P, NB])
        dinv = sb("dinv", [P, NB])
        scratch = sb("scratch", [P, 1])
        y = sb("y", [P, D])
        hm = sb("hm", [P, D])
        hmT = sb("hmT", [P, KD, P])
        th = sb("th", [P, D])
        obuf = sb("obuf", [P, 2, D])
        w1_sb = obuf
        b0_row, b1_row = y[0:1, :], hm[0:1, :]
        xg = [A[:, b, 0:GR * D].rearrange("p (r d) -> p r d", r=GR) for b in range(2)]
        xT = [M[:, b, 0:KD * CH].rearrange("p (k n) -> p k n", k=KD) for b in range(2)]

        E4 = psum("E4", [P, 4 * CH])
        E = [E4[:, i * CH:(i + 1) * CH] for i in range(4)]
        EA, EB = E4[:, 0:2 * CH], E4[:, 2 * CH:4 * CH]
        T = [psum(f"T{i}", [P, CH]) for i in range(2)]
        O = [psum(f"O{i}", [P, CH]) for i in range(2)]
        S4 = T + O

        w_loaded = sem("w_loaded")
        x1_loaded = sem("x1_loaded")
        xg_loaded = [sem(f"xg_loaded{i}") for i in range(2)]
        a_loaded = [sem(f"a_loaded{i}") for i in range(2)]
        ident_zero = sem("ident_zero")
        consts = sem("consts")
        bias_ready = sem("bias_ready")
        bias_copied = sem("bias_copied")
        wt_ready = sem("wt_ready")
        wt_copied = sem("wt_copied")
        xt_ready = sem("xt_ready")
        xt_copied_act = sem("xt_copied_act")
        xt_copied_dve = sem("xt_copied_dve")
        h_ready = sem("h_ready")
        h_copied = sem("h_copied")
        sup_ready = sem("sup_ready")
        sup_copied = sem("sup_copied")
        node_dve = sem("node_dve")
        node_pool = sem("node_pool")
        node_act = sem("node_act")
        att_ready = sem("att_ready")
        hi_staged = sem("hi_staged")
        x_biased = sem("x_biased")
        a_summed = sem("a_summed")
        a_used = sem("a_used")
        e_ready = sem("e_ready")
        e_masked = sem("e_masked")
        negmax_ready = sem("negmax_ready")
        exp_done = sem("exp_done")
        p_ready = sem("p_ready")
        t_ready = sem("t_ready")
        t_copied = sem("t_copied")
        pv_done = sem("pv_done")
        o_read = sem("o_read")
        deg_ready = sem("deg_ready")
        g_ready = sem("g_ready")
        hm_ready = sem("hm_ready")
        hmt_ready = sem("hmt_ready")
        hmt_copied = sem("hmt_copied")
        lin_ready = sem("lin_ready")
        lin_biased = sem("lin_biased")
        tanh_done = sem("tanh_done")
        y_ready = sem("y_ready")
        stored = [sem(f"stored{i}") for i in range(2)]
        dve_chain = sem("dve_chain")

        x_groups = x.rearrange("(g r p) d -> g p r d", p=P, r=GR)
        x_rows = x.rearrange("(b p) d -> p b d", p=P)
        adj_rows = adj.rearrange("(b p) n -> b p n", p=P)
        out_rows = out.rearrange("(b p) d -> b p d", p=P)

        block = ctx.enter_context(nc.Block())

        @block.sync
        def _(sp):
            with sp.If(sp.value_load(flag[0:1, 0:1], min_val=0, max_val=1) != 0):
                sp.dma_start(edge_sb[:, :, :], edge_w.rearrange("(k p) d -> p k d", p=P)).then_inc(w_loaded, 16)
                sp.dma_start(w0n[:, :, 0:D], w0.rearrange("(k p) d -> p k d", p=P)).then_inc(w_loaded, 16)
                sp.dma_start(w0n[:, :, D:D + 1], node_w.rearrange("(k p) d -> p k d", p=P),
                             allow_slow_non_contiguous=True).then_inc(w_loaded, 16)
                sp.dma_start(w1_sb[:, :, :], w1.rearrange("(k p) d -> p k d", p=P)).then_inc(w_loaded, 16)
                sp.dma_start(b0_row[:, :], b0.rearrange("(a d) -> a d", a=1)).then_inc(w_loaded, 16)
                sp.dma_start(b1_row[:, :], b1.rearrange("(a d) -> a d", a=1)).then_inc(w_loaded, 16)
                for g in range(2):
                    sp.dma_start(xg[g], x_groups[g]).then_inc(xg_loaded[g], 16)
                with sp.Fori(2, NG - 1, 2) as g0:
                    for b in range(2):
                        g = g0 + b
                        sp.wait_ge(xt_ready, g - 1)
                        sp.dma_start(xg[b], x_groups[bass.ds(g, 1)].rearrange("a p r d -> (a p) r d")
                                     ).then_inc(xg_loaded[b], 16)
                sp.dma_start(x1[:, :, :], x_rows).then_inc(x1_loaded, 16)
                sp.wait_ge(xt_ready, NG)
                for b in range(2):
                    sp.dma_start(A[:, b, :], adj_rows[b]).then_inc(a_loaded[b], 16)
                with sp.Fori(2, NB - 1, 2) as i0:
                    for b in range(2):
                        i = i0 + b
                        sp.wait_ge(a_used, i - 1)
                        sp.wait_ge(a_summed, i - 1)
                        sp.dma_start(A[:, b, :], adj_rows[bass.ds(i, 1)].rearrange("a p n -> (a p) n")
                                     ).then_inc(a_loaded[b], 16)
                for b in range(2):
                    sp.wait_ge(a_used, NB - 1 + b)
                    sp.wait_ge(a_summed, NB - 1 + b)
                    sp.dma_start(A[:, b, :], adj_rows[b]).then_inc(a_loaded[b], 16)
                with sp.Fori(0, NB - 3, 2) as j0:
                    for b in range(2):
                        j = j0 + b
                        sp.wait_ge(t_ready, C * (NB + 1) + C * j)
                        sp.dma_start(A[:, b, :], adj_rows[bass.ds(j + 2, 1)].rearrange("a p n -> (a p) n")
                                     ).then_inc(a_loaded[b], 16)
                        sp.wait_ge(y_ready, j + 1)
                        sp.dma_start(out_rows[bass.ds(j, 1)].rearrange("a p d -> (a p) d"), obuf[:, b, :]
                                     ).then_inc(stored[b], 16)
                for b in range(2):
                    sp.wait_ge(y_ready, NB - 1 + b)
                    sp.dma_start(out_rows[NB - 2 + b], obuf[:, b, :]).then_inc(stored[b], 16)
                for b in range(2):
                    sp.wait_ge(stored[b], 16 * (NB // 2))

        @block.tensor
        def _(pe):
            with pe.If(pe.value_load(flag[0:1, 0:1], min_val=0, max_val=1) != 0):
                pe.wait_ge(consts, 3)
                pe.wait_ge(w_loaded, 96)
                nc.tensor.matmul(O[0][:, 0:D], ones[0:1, :], b0_row[:, :], start=True, stop=True)
                nc.tensor.matmul(O[1][:, 0:D], ones[0:1, :], b1_row[:, :], start=True, stop=True
                                 ).then_inc(bias_ready, 1)
                for k in range(KD):
                    for o in range(KD):
                        last = nc.tensor.transpose(T[0][:, (k * KD + o) * P:(k * KD + o + 1) * P],
                                                   w1_sb[:, o, k * P:(k + 1) * P], ident[:, :])
                last.then_inc(wt_ready, 1)

                def transpose_group(g, b):
                    pe.wait_ge(xg_loaded[b], 8 * (g - b) + 16)
                    for k in range(KD):
                        for r in range(GR):
                            last = nc.tensor.transpose(EA[:, k * CH + r * P:k * CH + (r + 1) * P],
                                                       xg[b][:, r, k * P:(k + 1) * P], ident[:, :])
                    last.then_inc(xt_ready, 1)

                def project_group(g, b, first=False):
                    pe.wait_ge(xt_copied_act, g + 1)
                    pe.wait_ge(xt_copied_dve, g + 1)
                    if not first:
                        pe.wait_ge(h_copied, g)
                    for m in range(KD):
                        for k in range(KD):
                            last = nc.tensor.matmul(EB[:, m * CH:(m + 1) * CH], edge_sb[:, k, m * P:(m + 1) * P],
                                                    xT[b][:, k, :], start=(k == 0), stop=(k == KD - 1))
                    last.then_inc(h_ready, 1)
                    if not first:
                        pe.wait_ge(sup_copied, g)
                    for r in range(GR):
                        for k in range(KD):
                            last = nc.tensor.matmul(S4[r][:, 0:D + 1], xT[b][:, k, r * P:(r + 1) * P], w0n[:, k, :],
                                                    start=(k == 0), stop=(k == KD - 1))
                    last.then_inc(sup_ready, 1)

                def next_transpose(g, b):
                    pe.wait_ge(xt_copied_act, g)
                    pe.wait_ge(xt_copied_dve, g)
                    transpose_group(g, b)

                transpose_group(0, 0)
                pe.wait_ge(bias_copied, 1)
                pe.wait_ge(wt_copied, 1)
                next_transpose(1, 1)
                project_group(0, 0, first=True)
                next_transpose(2, 0)
                project_group(1, 1)
                with pe.Fori(2, NG - 3, 2) as g0:
                    for b in range(2):
                        next_transpose(g0 + b + 1, (b + 1) % 2)
                        project_group(g0 + b, b)
                next_transpose(NG - 1, 1)
                project_group(NG - 2, 0)
                project_group(NG - 1, 1)

                def scores(i, b, first=False):
                    pe.wait_ge(hi_staged, i + 1)
                    for u in range(U):
                        if not (first and u < 4):
                            pe.wait_ge(e_masked, U * i + u - 3)
                        for k in range(KD):
                            last = nc.tensor.matmul(E[u % 4], hI[:, b, k, :], hT[:, k, u * UN:(u + 1) * UN],
                                                    start=(k == 0), stop=(k == KD - 1))
                        last.then_inc(e_ready, 1)

                def transpose_chunk(n, c, src, first=False):
                    if not (first and c < 2):
                        pe.wait_ge(t_copied, C * n + c - 1)
                    for t in range(TJ):
                        col = c * CH + t * P
                        last = nc.tensor.transpose(T[c % 2][:, t * P:(t + 1) * P], src[:, col:col + P], ident[:, :])
                    last.then_inc(t_ready, 1)

                def product_chunk(n, b, c):
                    pe.wait_ge(t_copied, C * n + c + 1)
                    for t in range(TJ):
                        last = nc.tensor.matmul(O[b][:, 0:D], PT[:, c % 4, t * P:(t + 1) * P], sup[:, c * TJ + t, :],
                                                start=(c == 0 and t == 0), stop=(c == C - 1 and t == TJ - 1))
                    last.then_inc(pv_done, 1)

                def attend(i, b, first=False):
                    for c in range(C):
                        pe.wait_ge(p_ready, U * i + c + 1)
                        transpose_chunk(i, c, M[:, b, :], first)
                        if c == 1 and not first:
                            pe.wait_ge(o_read, i - 1)
                        if c > 0:
                            product_chunk(i, b, c - 1)
                    product_chunk(i, b, C - 1)

                pe.wait_ge(h_copied, NG)
                pe.wait_ge(sup_copied, NG)
                scores(0, 0, first=True)
                scores(1, 1)
                attend(0, 0, first=True)
                scores(2, 0)
                attend(1, 1)
                with pe.Fori(2, NB - 3, 2) as i0:
                    for b in range(2):
                        scores(i0 + b + 1, (b + 1) % 2)
                        attend(i0 + b, b)
                scores(NB - 1, 1)
                attend(NB - 2, 0)
                attend(NB - 1, 1)

                pe.wait_ge(a_summed, NB)
                for t in range(NB):
                    last = nc.tensor.matmul(E[0][:, t:t + 1], colsum[:, t * P:(t + 1) * P], ones[:, 0:1],
                                            start=True, stop=True)
                last.then_inc(deg_ready, 1)

                def hm_transpose(j):
                    pe.wait_ge(hm_ready, j + 1)
                    for k in range(KD):
                        last = nc.tensor.transpose(E[0][:, k * P:(k + 1) * P], hm[:, k * P:(k + 1) * P], ident[:, :])
                    last.then_inc(hmt_ready, 1)

                def hm_linear(j):
                    pe.wait_ge(hmt_copied, j + 1)
                    pe.wait_ge(lin_biased, j)
                    for k in range(KD):
                        last = nc.tensor.matmul(E[1][:, 0:D], hmT[:, k, :], w1T[:, k, :],
                                                start=(k == 0), stop=(k == KD - 1))
                    last.then_inc(lin_ready, 1)

                def aggregate(j, b, first=False):
                    n = NB + j
                    pe.wait_ge(a_loaded[b], 16 * (NB // 2) + 8 * (j - b) + 16)
                    for c in range(C):
                        transpose_chunk(n, c, A[:, b, :])
                        if c == 1:
                            pe.wait_ge(o_read, n - 1)
                        if c > 0:
                            if first:
                                pe.wait_ge(g_ready, TJ * c)
                            product_chunk(n, b, c - 1)
                        if c == 3 and not first:
                            hm_transpose(j - 1)
                        if c == 5 and not first:
                            hm_linear(j - 1)
                    if first:
                        pe.wait_ge(g_ready, NB)
                    product_chunk(n, b, C - 1)

                aggregate(0, 0, first=True)
                aggregate(1, 1)
                with pe.Fori(2, NB - 1, 2) as j0:
                    for b in range(2):
                        aggregate(j0 + b, b)
                hm_transpose(NB - 1)
                hm_linear(NB - 1)

        @block.gpsimd
        def _(pool):
            with pool.If(pool.value_load(flag[0:1, 0:1], min_val=0, max_val=1) != 0):
                nc.gpsimd.memset(ident[:, :], 0.0).then_inc(ident_zero, 1)
                nc.gpsimd.memset(ones[:, :], 1.0).then_inc(consts, 1)
                pool.wait_ge(ident_zero, 1)
                nc.gpsimd.affine_select(out=ident[:, :], in_=ident[:, :], compare_op=ALU.not_equal, fill=1.0, base=0,
                                        pattern=[[-1, P]], channel_multiplier=1).then_inc(consts, 1)
                nc.gpsimd.memset(colsum[:, :], 0.0).then_inc(consts, 1)
                pool.wait_ge(bias_copied, 1)
                pool.wait_ge(x1_loaded, 16)
                pool.wait_ge(h_copied, NG)

                def stage(i, b):
                    nc.gpsimd.tensor_copy(hI[:, b, :, :], hT[:, :, bass.ds(i * P, P)]).then_inc(hi_staged, 1)

                def add_bias(i):
                    nc.gpsimd.tensor_tensor(x1[:, bass.ds(i, 1), :].rearrange("p a d -> p (a d)"),
                                            x1[:, bass.ds(i, 1), :].rearrange("p a d -> p (a d)"), b0_sb[:, :],
                                            ALU.add).then_inc(x_biased, 1)

                def add_columns(i, b, first=False):
                    pool.wait_ge(a_loaded[b], 8 * (i - b) + 16)
                    if not first:
                        pool.wait_ge(a_summed, i)
                    nc.gpsimd.tensor_tensor(colsum[:, :], colsum[:, :], A[:, b, :], ALU.add).then_inc(a_summed, 1)

                stage(0, 0)
                stage(1, 1)
                pool.wait_ge(node_dve, 1)
                nc.gpsimd.partition_all_reduce(small[:, 1:2], small[:, 0:1], P, RMAX).then_inc(node_pool, 1)
                pool.wait_ge(node_act, 1)
                nc.gpsimd.partition_all_reduce(small[:, 4:5], small[:, 3:4], P, RADD).then_inc(node_pool, 1)
                pool.wait_ge(consts, 3)
                add_bias(0)
                add_columns(0, 0, first=True)
                add_bias(1)
                add_columns(1, 1)
                with pool.Fori(2, NB - 1, 2) as i0:
                    for b in range(2):
                        i = i0 + b
                        pool.wait_ge(e_ready, U * (i - 1))
                        stage(i, b)
                        add_bias(i)
                        add_columns(i, b)

        @block.scalar
        def _(act):
            with act.If(act.value_load(flag[0:1, 0:1], min_val=0, max_val=1) != 0):
                act.wait_ge(bias_ready, 1)
                nc.scalar.copy(b0_sb[:, :], O[0][:, 0:D])
                nc.scalar.copy(b1_sb[:, :], O[1][:, 0:D]).then_inc(bias_copied, 1)
                act.wait_ge(wt_ready, 1)
                nc.scalar.copy(w1T[:, :, :], T[0][:, :].rearrange("p (k n) -> p k n", k=KD)).then_inc(wt_copied, 1)

                def copy_group(g, b, first=False):
                    act.wait_ge(xt_ready, g + 1)
                    if not first:
                        act.wait_ge(sup_ready, g - 1)
                    nc.scalar.copy(xT[b][:, 0, :], EA[:, 0:CH]).then_inc(xt_copied_act, 1)

                def copy_h(g):
                    act.wait_ge(h_ready, g + 1)
                    nc.scalar.copy(hT[:, :, bass.ds(g * CH, CH)], EB.rearrange("p (k n) -> p k n", k=KD)
                                   ).then_inc(h_copied, 1)

                copy_group(0, 0, first=True)
                copy_group(1, 1, first=True)
                with act.Fori(0, NG - 3, 2) as g0:
                    for b in range(2):
                        copy_h(g0 + b)
                        copy_group(g0 + b + 2, b)
                copy_h(NG - 2)
                copy_h(NG - 1)
                act.wait_ge(node_dve, 2)
                nc.scalar.activation(att[:, :], logits[:, :], ACT.Exp, bias=small[:, 2:3], scale=1.0,
                                     accum_out=small[:, 3:4]).then_inc(node_act, 1)

                def exps(i, b, u):
                    if u == 0:
                        act.wait_ge(negmax_ready, i + 1)
                    nc.scalar.activation(M[:, b, u * UN:(u + 1) * UN], M[:, b, u * UN:(u + 1) * UN], ACT.Exp,
                                         bias=negmax[:, b:b + 1], scale=1.0,
                                         accum_out=unitsum[:, b, u:u + 1]).then_inc(exp_done, 1)

                def copy_transposed(n, c, first=False):
                    act.wait_ge(t_ready, C * n + c + 1)
                    if not (first and c < 4):
                        act.wait_ge(pv_done, C * n + c - 3)
                    nc.scalar.copy(PT[:, c % 4, :], T[c % 2][:, :]).then_inc(t_copied, 1)

                def attend(i, b, first=False, last=False):
                    for c in range(C):
                        copy_transposed(i, c, first)
                        if not last:
                            exps(i + 1, (b + 1) % 2, c)

                for u in range(U):
                    exps(0, 0, u)
                attend(0, 0, first=True)
                attend(1, 1)
                with act.Fori(2, NB - 3, 2) as i0:
                    for b in range(2):
                        attend(i0 + b, b)
                attend(NB - 2, 0)
                attend(NB - 1, 1, last=True)

                def aggregate(j, first=False):
                    for c in range(C):
                        copy_transposed(NB + j, c)
                        if c == 4 and not first:
                            copy_hmT(j - 1)
                        if c == 7 and not first:
                            tanh(j - 1)

                def copy_hmT(j):
                    act.wait_ge(hmt_ready, j + 1)
                    nc.scalar.copy(hmT[:, :, :], E[0][:, 0:D].rearrange("p (k n) -> p k n", k=KD)
                                   ).then_inc(hmt_copied, 1)

                def tanh(j):
                    act.wait_ge(lin_biased, j + 1)
                    nc.scalar.activation(th[:, :], th[:, :], ACT.Tanh).then_inc(tanh_done, 1)

                aggregate(0, first=True)
                with act.Fori(1, NB, 1) as j:
                    aggregate(j)
                copy_hmT(NB - 1)
                tanh(NB - 1)

        @block.vector
        def _(dve):
            with dve.If(dve.value_load(flag[0:1, 0:1], min_val=0, max_val=1) != 0):
                links = [0]

                def link(ins):
                    links[0] = links[0] + 1
                    ins.then_inc(dve_chain, 1)
                    dve.wait_ge(dve_chain, links[0])

                def carry_wait():
                    nc.vector.memset(scratch[:, :], 0.0)

                def rsqrt(v, r, t):
                    link(nc.vector.tensor_scalar(r.bitcast(I32), v.bitcast(I32), -0.5, float(RSQRT_SEED),
                                                 ALU.mult, ALU.add))
                    for _ in range(RSQRT_STEPS):
                        link(nc.vector.scalar_tensor_tensor(out=t, in0=r, scalar=-0.5, in1=r, op0=ALU.mult,
                                                            op1=ALU.mult))
                        link(nc.vector.tensor_tensor(t, t, v, ALU.mult))
                        link(nc.vector.scalar_tensor_tensor(out=r, in0=t, scalar=1.5, in1=r, op0=ALU.add,
                                                            op1=ALU.mult))

                def copy_group(g, b, first=False):
                    dve.wait_ge(xt_ready, g + 1)
                    if not first:
                        dve.wait_ge(sup_ready, g - 1)
                    nc.vector.tensor_copy(xT[b][:, 1, :], EA[:, CH:2 * CH]).then_inc(xt_copied_dve, 1)

                def copy_support(g):
                    dve.wait_ge(sup_ready, g + 1)
                    for r in range(GR):
                        nc.vector.tensor_copy(sup[:, bass.ds(g * GR + r, 1), :].rearrange("p a d -> p (a d)"),
                                              S4[r][:, 0:D])
                        last = nc.vector.tensor_copy(logits[:, bass.ds(g * GR + r, 1)], S4[r][:, D:D + 1])
                    last.then_inc(sup_copied, 1)

                copy_group(0, 0, first=True)
                copy_group(1, 1, first=True)
                with dve.Fori(0, NG - 3, 2) as g0:
                    for b in range(2):
                        copy_support(g0 + b)
                        copy_group(g0 + b + 2, b)
                copy_support(NG - 2)
                copy_support(NG - 1)

                def mask_and_max(i, b):
                    dve.wait_ge(a_loaded[b], 8 * (i - b) + 16)
                    def mask(u):
                        return nc.vector.tensor_scalar(negs[:, u % 2, :], A[:, b, u * UN:(u + 1) * UN], 0.0, NEG_BIG,
                                                       ALU.is_le, ALU.mult)

                    dve.wait_ge(e_masked, U * i)
                    ins = mask(0)
                    for u in range(U):
                        link(ins)
                        dve.wait_ge(e_ready, U * i + u + 1)
                        dve.wait_ge(e_masked, U * i + u)
                        if u + 1 < U:
                            ins = mask(u + 1)
                        else:
                            carry_wait()
                        nc.vector.tensor_tensor_reduce(
                            out=M[:, b, u * UN:(u + 1) * UN], in0=E[u % 4], in1=negs[:, u % 2, :], scale=1.0,
                            scalar=-3.0e38, op0=ALU.add, op1=ALU.max, accum_out=unitmax[:, u:u + 1]
                        ).then_inc(e_masked, 1)
                    dve.wait_ge(e_masked, U * i + U)
                    nc.vector.tensor_reduce(negmax[:, b:b + 1], unitmax[:, :], AX.X, ALU.max, negate=True
                                            ).then_inc(negmax_ready, 1)

                def weigh(i, b):
                    for u in range(U):
                        dve.wait_ge(exp_done, U * i + u + 1)
                        cols = slice(u * UN, (u + 1) * UN)
                        ins = nc.vector.tensor_tensor(M[:, b, cols], M[:, b, cols], A[:, b, cols], ALU.mult)
                        ins.then_inc(p_ready, 1)
                    dve.wait_ge(p_ready, U * i + U)
                    nc.vector.sem_inc(a_used, 1)

                def normalise(dst):
                    link(nc.vector.bn_stats(stats[:, :], y[:, :]))
                    carry_wait()
                    link(nc.vector.bn_aggr(meanvar[:, :], stats[:, :]))
                    link(nc.vector.tensor_scalar(nv[:, 0:1], meanvar[:, 1:2], EPS, None, ALU.add))
                    rsqrt(nv[:, 0:1], ny[:, 0:1], nt[:, 0:1])
                    return nc.vector.tensor_scalar(dst, y[:, :], meanvar[:, 0:1], ny[:, 0:1], ALU.subtract, ALU.mult)

                def finish_first(i, b):
                    link(nc.vector.tensor_reduce(rowscale[:, 0:1], unitsum[:, b, :], AX.X, ALU.add))
                    link(nc.vector.reciprocal(rowscale[:, 1:2], rowscale[:, 0:1]))
                    link(nc.vector.tensor_tensor(rowscale[:, 2:3], rowscale[:, 1:2], att[:, bass.ds(i, 1)], ALU.mult))
                    dve.wait_ge(pv_done, C * (i + 1))
                    dve.wait_ge(x_biased, i + 1)
                    row = x1[:, bass.ds(i, 1), :].rearrange("p a d -> p (a d)")
                    nc.vector.scalar_tensor_tensor(out=y[:, :], in0=O[b][:, 0:D], scalar=rowscale[:, 2:3], in1=row,
                                                   op0=ALU.mult, op1=ALU.add).then_inc(o_read, 1)
                    dve.wait_ge(o_read, i + 1)
                    link(normalise(row))

                dve.wait_ge(sup_copied, NG)
                nc.vector.tensor_reduce(small[:, 0:1], logits[:, :], AX.X, ALU.max).then_inc(node_dve, 1)
                dve.wait_ge(node_pool, 1)
                nc.vector.tensor_scalar(small[:, 2:3], small[:, 1:2], -1.0, None, ALU.mult).then_inc(node_dve, 1)
                dve.wait_ge(node_pool, 2)
                link(nc.vector.reciprocal(small[:, 5:6], small[:, 4:5]))
                link(nc.vector.tensor_scalar(att[:, :], att[:, :], small[:, 5:6], None, ALU.mult))

                mask_and_max(0, 0)
                weigh(0, 0)

                def step(i, b):
                    mask_and_max(i + 1, (b + 1) % 2)
                    weigh(i + 1, (b + 1) % 2)
                    finish_first(i, b)

                step(0, 0)
                before = links[0]
                step(1, 1)
                per_step = links[0] - before
                with dve.Fori(2, NB - 3, 2) as i0:
                    for b in range(2):
                        links[0] = before + per_step * (i0 + b - 1)
                        step(i0 + b, b)
                links[0] = before + per_step * (NB - 3)
                step(NB - 2, 0)
                finish_first(NB - 1, 1)

                dve.wait_ge(deg_ready, 1)
                link(nc.vector.tensor_scalar(nv[:, :], E[0][:, 0:NB], 1.0, None, ALU.add))
                rsqrt(nv[:, :], ny[:, :], nt[:, :])
                link(nc.vector.tensor_scalar(nt[:, :], nv[:, :], 0.0, None, ALU.not_equal))
                link(nc.vector.tensor_tensor(dinv[:, :], ny[:, :], nt[:, :], ALU.mult))
                with dve.Fori(0, NB, 1) as j:
                    nc.vector.tensor_scalar(sup[:, bass.ds(j, 1), :].rearrange("p a d -> p (a d)"),
                                            x1[:, bass.ds(j, 1), :].rearrange("p a d -> p (a d)"),
                                            dinv[:, bass.ds(j, 1)], None, ALU.mult).then_inc(g_ready, 1)
                dve.wait_ge(g_ready, NB)

                def scale_rows(j, b):
                    dve.wait_ge(pv_done, C * (NB + 1) + C * j)
                    dve.wait_ge(y_ready, j)
                    g = sup[:, bass.ds(j, 1), :].rearrange("p a d -> p (a d)")
                    nc.vector.tensor_tensor(y[:, :], O[b][:, 0:D], g, ALU.add).then_inc(o_read, 1)
                    dve.wait_ge(o_read, NB + j + 1)
                    nc.vector.tensor_scalar(hm[:, :], y[:, :], dinv[:, bass.ds(j, 1)], None, ALU.mult
                                            ).then_inc(hm_ready, 1)

                def bias_linear(j):
                    dve.wait_ge(lin_ready, j + 1)
                    nc.vector.tensor_tensor(th[:, :], E[1][:, 0:D], b1_sb[:, :], ALU.add).then_inc(lin_biased, 1)

                def finish_second(j, b, first=False):
                    dve.wait_ge(tanh_done, j + 1)
                    if not first:
                        dve.wait_ge(stored[b], 8 * (j - b))
                    row = x1[:, bass.ds(j, 1), :].rearrange("p a d -> p (a d)")
                    link(nc.vector.tensor_tensor(y[:, :], th[:, :], row, ALU.add))
                    normalise(obuf[:, b, :]).then_inc(y_ready, 1)

                def tail(j, b, first=False):
                    bias_linear(j)
                    finish_second(j, b, first)

                scale_rows(0, 0)
                tail(0, 0, first=True)
                scale_rows(1, 1)
                before2 = links[0]
                tail(1, 1, first=True)
                per_tail = links[0] - before2
                with dve.Fori(2, NB - 1, 2) as j0:
                    for b in range(2):
                        scale_rows(j0 + b, b)
                        links[0] = before2 + per_tail * (j0 + b - 1)
                        tail(j0 + b, b)


def build(nc, x, adj, w0, b0, node_w, edge_w, w1, b1, out):
    adj16 = nc.dram_tensor("adj16", adj.shape, F16).ap()
    with nc.sbuf_tensor("flag", [P, 1], I32) as flag:
        split_path(nc, flag, adj16, x, adj, w0, b0, node_w, edge_w, w1, b1, out)
        general_path(nc, flag, x, adj, w0, b0, node_w, edge_w, w1, b1, out)


_INS = ['x', 'adj', 'L0_gnn_weight', 'L0_gnn_bias', 'L0_gnn_node_w', 'L0_gnn_edge_w', 'L1_gnn_W', 'L1_gnn_b']
_OUTS = [((4096, 256), 'float32')]


def kernel(**inputs):
    import numpy as _np
    import concourse.bacc as _bacc
    from concourse import mybir as _mybir
    from concourse.bass_utils import run_bass_kernel_spmd as _run

    nc = _bacc.Bacc("TRN2", target_bir_lowering=False, num_devices=1)
    arrays, args = {}, []
    for name in _INS:
        a = _np.ascontiguousarray(inputs[name])
        arrays[f"in_{name}_dram"] = a
        args.append(nc.dram_tensor(f"in_{name}_dram", a.shape, _mybir.dt.from_np(a.dtype), kind="ExternalInput").ap())
    for i, (shape, dtype) in enumerate(_OUTS):
        dt = _mybir.dt.from_np(_np.dtype(dtype))
        args.append(nc.dram_tensor(f"out_{i}_dram", shape, dt, kind="ExternalOutput").ap())
    build(nc, *args)
    r = _run(nc, [arrays], core_ids=[0])
    got = tuple(r.results[0][f"out_{i}_dram"] for i in range(len(_OUTS)))
    return got[0]
```

```python
from contextlib import ExitStack

import concourse.bass as bass
from concourse import mybir

P = 128
ALU = mybir.AluOpType
ACT = mybir.ActivationFunctionType
AX = mybir.AxisListType
F32 = mybir.dt.float32
I32 = mybir.dt.int32
F16 = mybir.dt.float16
BF16 = mybir.dt.bfloat16
RMAX = bass.bass_isa.ReduceOp.max
RADD = bass.bass_isa.ReduceOp.add

NEG_BIG = -9000000000000000.0
EPS = 1e-5
RSQRT_SEED = 0x5F3759DF
RSQRT_STEPS = 3


X_SCALE = 256.0
EDGE_SCALE = 256.0
W0_SCALE = 16.0
P_SCALE = 4096.0
G_SCALE = 2048.0


def rows(t, i):
    return t[:, bass.ds(i, 1), :].rearrange("p a d -> p (a d)")

def split_path(nc, flag, adj16, x, adj, w0, b0, node_w, edge_w, w1, b1, out):
    N, D = x.shape
    NB = N // P
    KD = D // P
    CH = 512
    PC = 2 * CH
    W = N // PC
    TW = PC // P
    HALF = N // 2
    HW = W // 2
    AB = 4
    LEAD = 6
    NM = 2
    GR = CH // P
    NG = NB // GR

    with ExitStack() as ctx:
        def sb(name, shape, dt=F32):
            return ctx.enter_context(nc.sbuf_tensor("s_" + name, shape, dt))

        def psum(name, shape, dt=F32):
            return ctx.enter_context(nc.psum_tensor("s_" + name, shape, dt))

        def sem(name):
            return ctx.enter_context(nc.semaphore("s_" + name))

        hT = sb("hT", [P, 2, KD, N], F16)
        sup = sb("sup", [P, NB, 2 * D], F16)
        x1 = sb("x1", [P, NB, D])
        A = sb("A", [P, 2, HALF])
        A16 = sb("A16", [P, 2, N], F16)
        M = sb("M", [P, 2, N])
        colsum = sb("colsum", [P, N], F16)
        negs = sb("negs", [P, NM, PC], BF16)
        X = sb("X", [P, 2 * PC], F16)
        PT = sb("PT", [P, W, 2 * PC], F16)
        hI = sb("hI", [P, 2, 2, KD, P], F16)
        w1T = sb("w1T", [P, KD, D])
        b0_sb = sb("b0_sb", [P, D])
        b1_sb = sb("b1_sb", [P, D])
        ident = sb("ident", [P, P])
        ones = sb("ones", [P, P])
        ones16 = sb("ones16", [P, 2], F16)
        unequal = sb("unequal", [P, NB * W])
        junk = sb("junk", [P, 2, PC], F16)
        h_guard = sb("h_guard", [P, NG])
        sup_guard = sb("sup_guard", [P, NB])
        guard = sb("guard", [P, 6])
        logits = sb("logits", [P, NB])
        att = sb("att", [P, NB])
        small = sb("small", [P, 8])
        piecemax = sb("piecemax", [P, W])
        negmax = sb("negmax", [P, 2])
        piecesum = sb("piecesum", [P, 2, W])
        rowscale = sb("rowscale", [P, 4])
        stats = sb("stats", [P, 6])
        meanvar = sb("meanvar", [P, 2])
        nv = sb("nv", [P, 1])
        nvh = sb("nvh", [P, 1])
        ny = sb("ny", [P, 1])
        nt = sb("nt", [P, 1])
        deg = sb("deg", [P, NB])
        dt = sb("dt", [P, NB])
        dinv = sb("dinv", [P, NB])
        dscaled = sb("dscaled", [P, NB])
        dunscaled = sb("dunscaled", [P, NB])
        scratch = sb("scratch", [P, W + 1])
        y = sb("y", [P, D])
        y2 = sb("y2", [P, D])
        HL = [[X[:, :] if w == 0 else M[:, b, (w - 1) * PC:w * PC].bitcast(F16) for w in range(W)]
              for b in range(2)]
        G = hT.rearrange("p s k n -> p (s k n)").rearrange("p (j d) -> p j d", d=2 * D)
        AT = M.rearrange("p b n -> p (b n)").bitcast(F16).rearrange("p (a n) -> p a n", a=AB)
        hm = A[:, 0, 0:D]
        hmT = A[:, 0, D:2 * D].rearrange("p (k n) -> p k n", k=KD)
        th = A[:, 0, 2 * D:3 * D]
        obuf = A[:, 1, 0:2 * D].rearrange("p (b d) -> p b d", b=2)
        edge_sb = PT[:, 0, :].bitcast(F32)[:, 0:KD * D].rearrange("p (k d) -> p k d", k=KD)
        w0n = PT[:, 1, :].bitcast(F32)[:, 0:KD * (D + 1)].rearrange("p (k d) -> p k d", k=KD)
        xg = [PT[:, 2 + b, :].bitcast(F32).rearrange("p (r d) -> p r d", r=GR) for b in range(2)]
        w1_sb = X.bitcast(F32)[:, 0:KD * D].rearrange("p (k d) -> p k d", k=KD)
        b0_row, b1_row = y[0:1, :], y2[0:1, :]
        xT = [M[:, b, 0:KD * CH].bitcast(F16).rearrange("p (s k n) -> p s k n", s=2, k=KD) for b in range(2)]
        edge16 = M[:, 0, 3 * PC:3 * PC + KD * D].bitcast(F16).rearrange("p (s k d) -> p s k d", s=2, k=KD)
        w0n16 = M[:, 1, 3 * PC:3 * PC + KD * (D + 1)].bitcast(F16).rearrange("p (s k d) -> p s k d", s=2, k=KD)

        NE = 3
        E6 = psum("E6", [P, NE * PC])
        E = [E6[:, i * PC:(i + 1) * PC] for i in range(NE)]
        O = [psum(f"O{i}", [P, CH]) for i in range(2)]
        EA, EB = E[0], E[1]
        S4 = [E[2][:, 0:CH], E[2][:, CH:PC]] + [o[:, :] for o in O]
        HT_BANK, LIN_BANK = E[0][:, 0:CH], E[0][:, CH:PC]

        w_loaded = sem("w_loaded")
        x1_loaded = sem("x1_loaded")
        xg_loaded = [sem(f"xg_loaded{i}") for i in range(2)]
        a_loaded = [sem(f"a_loaded{i}") for i in range(2)]
        a16_stored = [sem(f"a16_stored{i}") for i in range(2)]
        at_loaded = [sem(f"at_loaded{i}") for i in range(AB)]
        ident_zero = sem("ident_zero")
        consts = sem("consts")
        bias_ready = sem("bias_ready")
        bias_copied = sem("bias_copied")
        wt_ready = sem("wt_ready")
        wt_copied = sem("wt_copied")
        xt_ready = sem("xt_ready")
        w_high = sem("w_high")
        w_split = sem("w_split")
        xt_high = sem("xt_high")
        xt_split = sem("xt_split")
        h_ready = sem("h_ready")
        h_high = sem("h_high")
        h_split = sem("h_split")
        sup_ready = sem("sup_ready")
        sup_high = sem("sup_high")
        sup_split = sem("sup_split")
        node_dve = sem("node_dve")
        node_pool = sem("node_pool")
        node_act = sem("node_act")
        hi_staged = sem("hi_staged")
        x_biased = sem("x_biased")
        a16_ready = sem("a16_ready")
        a_checked = sem("a_checked")
        a16_summed = sem("a16_summed")
        negs_ready = sem("negs_ready")
        e_ready = sem("e_ready")
        e_masked = sem("e_masked")
        negmax_ready = sem("negmax_ready")
        p_ready = sem("p_ready")
        p_high = sem("p_high")
        p_split = sem("p_split")
        pt_loaded = [sem(f"pt_loaded{w}") for w in range(W)]
        pv_done = sem("pv_done")
        sp_passed = sem("sp_passed")
        o_read = sem("o_read")
        row_done = sem("row_done")
        deg_ready = sem("deg_ready")
        d_ready = sem("d_ready")
        g_high = sem("g_high")
        g_split = sem("g_split")
        ag_done = sem("ag_done")
        o2_read = sem("o2_read")
        hm_ready = sem("hm_ready")
        hmt_ready = sem("hmt_ready")
        hmt_copied = sem("hmt_copied")
        lin_ready = sem("lin_ready")
        lin_biased = sem("lin_biased")
        tanh_done = sem("tanh_done")
        y_ready = sem("y_ready")
        stored = [sem(f"stored{i}") for i in range(2)]
        bad_rows = sem("bad_rows")
        bad_all = sem("bad_all")
        flag_ready = sem("flag_ready")
        dve_chain = sem("dve_chain")

        x_groups = x.rearrange("(g r p) d -> g p r d", p=P, r=GR)
        x_rows = x.rearrange("(b p) d -> p b d", p=P)
        adj_halves = adj.rearrange("(b p) (h n) -> b h p n", p=P, h=2)
        adj16_rows = adj16.rearrange("(b p) n -> b p n", p=P)
        out_rows = out.rearrange("(b p) d -> b p d", p=P)

        block = ctx.enter_context(nc.Block())

        @block.sync
        def _(sp):
            def load_group(g):
                sp.dma_start(xg[g % 2], x_groups[g]).then_inc(xg_loaded[g % 2], 16)

            def refill_adj(i, h, source):
                sp.wait_ge(a_checked, W * i + HW * (h + 1))
                sp.wait_ge(a16_ready, W * i + HW * (h + 1))
                sp.dma_start(A[:, h, :], source).then_inc(a_loaded[h], 16)

            load_group(0)
            sp.dma_start(edge_sb[:, :, :], edge_w.rearrange("(k p) d -> p k d", p=P)).then_inc(w_loaded, 16)
            sp.dma_start(w0n[:, :, 0:D], w0.rearrange("(k p) d -> p k d", p=P)).then_inc(w_loaded, 16)
            sp.dma_start(w0n[:, :, D:D + 1], node_w.rearrange("(k p) d -> p k d", p=P),
                         allow_slow_non_contiguous=True).then_inc(w_loaded, 16)
            sp.dma_start(b0_row[:, :], b0.rearrange("(a d) -> a d", a=1)).then_inc(w_loaded, 16)
            sp.dma_start(b1_row[:, :], b1.rearrange("(a d) -> a d", a=1)).then_inc(w_loaded, 16)
            sp.dma_start(w1_sb[:, :, :], w1.rearrange("(k p) d -> p k d", p=P)).then_inc(w_loaded, 16)
            load_group(1)
            for h in range(2):
                sp.dma_start(A[:, h, :], adj_halves[0, h]).then_inc(a_loaded[h], 16)
            for g in range(2, NG):
                sp.wait_ge(xt_ready, g - 1)
                load_group(g)
                if g >= NG - 2:
                    refill_adj(0, g - NG + 2, adj_halves[1, g - NG + 2])
            sp.dma_start(x1[:, :, :], x_rows).then_inc(x1_loaded, 16)

            def transpose_piece(i, b, w, first=False):
                sp.wait_ge(p_split, W * i + w + 1)
                sp.sem_inc(sp_passed, 1)
                if not first:
                    sp.wait_ge(pv_done, W * i + w + 1 - W)
                    sp.sem_inc(sp_passed, 1)
                sp.dma_start_transpose(PT[:, w, :].rearrange("p (t r) -> p t r", r=P), HL[b][w]
                                       ).then_inc(pt_loaded[w], 16)

            sp.wait_ge(a16_ready, W)
            sp.dma_start(adj16_rows[0], A16[:, 0, :]).then_inc(a16_stored[0], 16)
            for h in range(2):
                refill_adj(1, h, adj_halves[2, h])
            for w in range(W):
                transpose_piece(0, 0, w, first=True)

            def step(i, b, source, dest):
                transpose_piece(i + 1, 1 - b, 0)
                sp.wait_ge(a16_ready, W * (i + 2))
                sp.dma_start(dest, A16[:, 1 - b, :]).then_inc(a16_stored[1 - b], 16)
                refill_adj(i + 2, 0, source(0))
                transpose_piece(i + 1, 1 - b, 1)
                transpose_piece(i + 1, 1 - b, 2)
                refill_adj(i + 2, 1, source(1))
                transpose_piece(i + 1, 1 - b, 3)

            with sp.Fori(0, NB - 5, 2) as i0:
                for b in range(2):
                    i = i0 + b
                    step(i, b, lambda h: adj_halves[bass.ds(i + 3, 1), h].rearrange("a p n -> (a p) n"),
                         adj16_rows[bass.ds(i + 1, 1)].rearrange("a p n -> (a p) n"))
            i = NB - 4
            step(i, 0, lambda h: adj_halves[i + 3, h], adj16_rows[i + 1])
            transpose_piece(NB - 2, 0, 0)
            for i in range(NB - 2, NB):
                sp.wait_ge(a16_ready, W * (i + 1))
                sp.dma_start(adj16_rows[i], A16[:, i % 2, :]).then_inc(a16_stored[i % 2], 16)
            for w in range(1, W):
                transpose_piece(NB - 2, 0, w)

            def load_transposed(k, source):
                sp.dma_start_transpose(AT[:, k, :].rearrange("p (t r) -> p t r", r=P), source
                                       ).then_inc(at_loaded[k], 16)

            for w in range(W):
                sp.wait_ge(pt_loaded[w], 16 * (NB - 1))
            sp.wait_ge(a16_stored[0], 8 * NB)
            load_transposed(0, adj16_rows[0])
            for w in range(W):
                transpose_piece(NB - 1, 1, w)
            sp.wait_ge(a16_stored[1], 8 * NB)
            load_transposed(1, adj16_rows[1])
            for w in range(W):
                sp.wait_ge(pt_loaded[w], 16 * NB)
            for k in range(AB // 2, AB):
                load_transposed(k, adj16_rows[k])
            with sp.Fori(0, NB - 2 * AB + 1, AB) as j0:
                for k in range(AB):
                    j = j0 + k
                    sp.wait_ge(ag_done, j + 1)
                    load_transposed(k, adj16_rows[bass.ds(j + AB, 1)].rearrange("a p n -> (a p) n"))
                    sp.wait_ge(y_ready, j + 1)
                    sp.dma_start(out_rows[bass.ds(j, 1)].rearrange("a p d -> (a p) d"), obuf[:, k % 2, :]
                                 ).then_inc(stored[k % 2], 16)
            for j in range(NB - AB, NB):
                sp.wait_ge(y_ready, j + 1)
                sp.dma_start(out_rows[j], obuf[:, j % 2, :]).then_inc(stored[j % 2], 16)
            for b in range(2):
                sp.wait_ge(stored[b], 16 * (NB // 2))

        @block.tensor
        def _(pe):
            pe.wait_ge(consts, 3)

            def transpose_group(g, b):
                pe.wait_ge(xg_loaded[b], 8 * (g - b) + 16)
                for k in range(KD):
                    for r in range(GR):
                        last = nc.tensor.transpose(EA[:, k * CH + r * P:k * CH + (r + 1) * P],
                                                   xg[b][:, r, k * P:(k + 1) * P], ident[:, :])
                last.then_inc(xt_ready, 1)

            def project_group(g, b, first=False):
                pe.wait_ge(xt_split, g + 1)
                if not first:
                    pe.wait_ge(h_split, g)
                terms = [(k, s, m) for k in range(KD) for s, m in ((0, 0), (0, 1), (1, 0))]
                for m in range(KD):
                    for n, (k, s, t) in enumerate(terms):
                        last = nc.tensor.matmul(EB[:, m * CH:(m + 1) * CH], edge16[:, s, k, m * P:(m + 1) * P],
                                                xT[b][:, t, k, :], start=(n == 0), stop=(n == len(terms) - 1))
                last.then_inc(h_ready, 1)
                if not first:
                    pe.wait_ge(sup_split, g)
                for r in range(GR):
                    for n, (k, s, t) in enumerate(terms):
                        last = nc.tensor.matmul(S4[r][:, 0:D + 1], xT[b][:, s, k, r * P:(r + 1) * P],
                                                w0n16[:, t, k, :], start=(n == 0), stop=(n == len(terms) - 1))
                last.then_inc(sup_ready, 1)

            def next_transpose(g, b):
                pe.wait_ge(xt_split, g)
                transpose_group(g, b)

            transpose_group(0, 0)
            pe.wait_ge(w_loaded, 96)
            nc.tensor.matmul(O[0][:, 0:D], ones[0:1, :], b0_row[:, :], start=True, stop=True)
            nc.tensor.matmul(O[1][:, 0:D], ones[0:1, :], b1_row[:, :], start=True, stop=True
                             ).then_inc(bias_ready, 1)
            for k in range(KD):
                for o in range(KD):
                    last = nc.tensor.transpose(S4[0][:, (k * KD + o) * P:(k * KD + o + 1) * P],
                                               w1_sb[:, o, k * P:(k + 1) * P], ident[:, :])
            last.then_inc(wt_ready, 1)
            next_transpose(1, 1)
            pe.wait_ge(bias_copied, 1)
            pe.wait_ge(wt_copied, 1)
            pe.wait_ge(w_split, 2)
            project_group(0, 0, first=True)
            next_transpose(2, 0)
            project_group(1, 1)
            with pe.Fori(2, NG - 3, 2) as g0:
                for b in range(2):
                    next_transpose(g0 + b + 1, (b + 1) % 2)
                    project_group(g0 + b, b)
            next_transpose(NG - 1, 1)
            project_group(NG - 2, 0)
            project_group(NG - 1, 1)

            def scores(i, b, first=False):
                pe.wait_ge(hi_staged, i + 1)
                if not first:
                    pe.wait_ge(e_masked, W * i)
                for w in range(W):
                    if first and w == 1:
                        pe.wait_ge(h_split, NG)
                    if first and w == 2:
                        pe.wait_ge(sup_split, NG)
                    if w >= NE:
                        pe.wait_ge(e_masked, W * i + w - NE + 1)
                    terms = [(k, s, m) for k in range(KD) for s, m in ((0, 0), (0, 1), (1, 0))]
                    for half in range(2):
                        col = w * PC + half * CH
                        for n, (k, s, m) in enumerate(terms):
                            last = nc.tensor.matmul(E[w % NE][:, half * CH:(half + 1) * CH], hI[:, b, s, k, :],
                                                    hT[:, m, k, col:col + CH],
                                                    start=(n == 0), stop=(n == len(terms) - 1))
                    last.then_inc(e_ready, 1)

            def product(i, b, first=False, with_degrees=False):
                if not first:
                    pe.wait_ge(o_read, i - 1)
                for w in range(W):
                    pe.wait_ge(pt_loaded[w], 16 * (i + 1))
                    for t in range(TW):
                        j = w * TW + t
                        nc.tensor.matmul(O[b][:, :], PT[:, w, t * P:(t + 1) * P], sup[:, j, :],
                                         start=(j == 0), stop=False)
                        last = nc.tensor.matmul(O[b][:, 0:D], PT[:, w, PC + t * P:PC + (t + 1) * P],
                                                sup[:, j, 0:D], start=False, stop=(j == NB - 1))
                    last.then_inc(pv_done, 1)
                    if with_degrees and w == 0:
                        degrees()

            def degrees():
                pe.wait_ge(a16_summed, NB)
                pe.wait_ge(e_masked, W * NB)
                for t in range(NB):
                    last = nc.tensor.matmul(HT_BANK[:, t:t + 1], colsum[:, t * P:(t + 1) * P], ones16[:, 0:1],
                                            start=True, stop=True)
                last.then_inc(deg_ready, 1)

            scores(0, 0, first=True)
            for i in range(2):
                scores(i + 1, 1 - i)
                product(i, i, first=(i == 0))
            with pe.Fori(2, NB - 3, 2) as i0:
                for b in range(2):
                    scores(i0 + b + 1, 1 - b)
                    product(i0 + b, b)
            scores(NB - 1, 1)
            product(NB - 2, 0, with_degrees=True)
            product(NB - 1, 1)

            def hm_transpose(j):
                pe.wait_ge(hm_ready, j + 1)
                for k in range(KD):
                    last = nc.tensor.transpose(HT_BANK[:, k * P:(k + 1) * P], hm[:, k * P:(k + 1) * P], ident[:, :])
                last.then_inc(hmt_ready, 1)

            def hm_linear(j, first=False):
                pe.wait_ge(hmt_copied, j + 1)
                if not first:
                    pe.wait_ge(lin_biased, j)
                for k in range(KD):
                    last = nc.tensor.matmul(LIN_BANK[:, 0:D], hmT[:, k, :], w1T[:, k, :],
                                            start=(k == 0), stop=(k == KD - 1))
                last.then_inc(lin_ready, 1)

            def aggregate_tile(k, jj):
                return nc.tensor.matmul(O[k % 2][:, :], AT[:, k, jj * P:(jj + 1) * P], G[:, jj, :],
                                        start=(jj == 0), stop=(jj == NB - 1))

            def aggregate(j, k, between):
                pe.wait_ge(at_loaded[k], 4 * (j - k) + 16)
                pe.wait_ge(o2_read, j - 1)
                for jj in range(NB):
                    last = aggregate_tile(k, jj)
                    for at, i, first in between:
                        if jj == at:
                            hm_transpose(i)
                        if jj == at + 4:
                            hm_linear(i, first)
                last.then_inc(ag_done, 1)

            pe.wait_ge(o_read, NB - 1)
            pe.wait_ge(at_loaded[0], 16)
            for jj in range(NB + LEAD):
                if jj < NB:
                    pe.wait_ge(g_split, jj + 1)
                    last = aggregate_tile(0, jj)
                if jj == NB - 1:
                    last.then_inc(ag_done, 1)
                if jj == LEAD:
                    pe.wait_ge(at_loaded[1], 16)
                    pe.wait_ge(o_read, NB)
                if jj >= LEAD:
                    last = aggregate_tile(1, jj - LEAD)
            last.then_inc(ag_done, 1)
            aggregate(2, 2, [(8, 0, True), (NB - 8, 1, False)])
            for j in range(3, AB):
                aggregate(j, j, [(8, j - 1, False)])
            with pe.Fori(AB, NB - AB + 1, AB) as j0:
                for k in range(AB):
                    aggregate(j0 + k, k, [(8, j0 + k - 1, False)])
            hm_transpose(NB - 1)
            hm_linear(NB - 1)

        @block.gpsimd
        def _(pool):
            nc.gpsimd.memset(ident[:, :], 0.0).then_inc(ident_zero, 1)
            nc.gpsimd.memset(ones[:, :], 1.0).then_inc(consts, 1)
            nc.gpsimd.memset(ones16[:, :], 1.0).then_inc(consts, 1)
            pool.wait_ge(ident_zero, 1)
            nc.gpsimd.affine_select(out=ident[:, :], in_=ident[:, :], compare_op=ALU.not_equal, fill=1.0, base=0,
                                    pattern=[[-1, P]], channel_multiplier=1).then_inc(consts, 1)
            nc.gpsimd.memset(guard[:, :], 0.0).then_inc(consts, 1)
            nc.gpsimd.memset(colsum[:, :], 0.0).then_inc(consts, 1)
            def add_bias(i):
                nc.gpsimd.tensor_tensor(rows(x1, i), rows(x1, i), b0_sb[:, :], ALU.add).then_inc(x_biased, 1)

            def convert(i, b, first=False):
                if not first:
                    pool.wait_ge(a16_stored[b], 8 * (i - b))
                    pool.wait_ge(negs_ready, W * (i - 1))
                    pool.wait_ge(a16_summed, i - 1)
                for h in range(2):
                    pool.wait_ge(a_loaded[h], 16 * (i + 1))
                    nc.gpsimd.tensor_tensor(A16[:, b, h * HALF:(h + 1) * HALF], A[:, h, :], A[:, h, :], ALU.mult
                                            ).then_inc(a16_ready, HW)

            def add_columns(i, b, first=False):
                pool.wait_ge(a16_ready, W * (i + 1))
                if not first:
                    pool.wait_ge(a16_summed, i)
                nc.gpsimd.tensor_tensor(colsum[:, :], colsum[:, :], A16[:, b, :], ALU.add).then_inc(a16_summed, 1)

            pool.wait_ge(consts, 5)
            convert(0, 0, first=True)
            add_columns(0, 0, first=True)
            convert(1, 1, first=True)
            add_columns(1, 1)
            pool.wait_ge(node_dve, 1)
            nc.gpsimd.partition_all_reduce(small[:, 1:2], small[:, 0:1], P, RMAX).then_inc(node_pool, 1)
            pool.wait_ge(node_act, 1)
            nc.gpsimd.partition_all_reduce(small[:, 4:5], small[:, 3:4], P, RADD).then_inc(node_pool, 1)
            pool.wait_ge(bias_copied, 1)
            pool.wait_ge(x1_loaded, 16)
            add_bias(0)
            add_bias(1)
            with pool.Fori(2, NB - 1, 2) as i0:
                for b in range(2):
                    i = i0 + b
                    convert(i, b)
                    add_bias(i)
                    add_columns(i, b)
            pool.wait_ge(bad_rows, 1)
            nc.gpsimd.partition_all_reduce(guard[:, 5:6], guard[:, 4:5], P, RMAX).then_inc(bad_all, 1)

        @block.scalar
        def _(act):
            def copy_group(g, b, first=False):
                act.wait_ge(xt_ready, g + 1)
                if not first:
                    act.wait_ge(sup_ready, g - 1)
                nc.scalar.activation(xT[b][:, 0, :, :], EA.rearrange("p (k n) -> p k n", k=KD), ACT.Copy,
                                     scale=X_SCALE).then_inc(xt_high, 1)

            def high_parts(g):
                act.wait_ge(h_ready, g + 1)
                nc.scalar.activation(hT[:, 0, :, bass.ds(g * CH, CH)], EB.rearrange("p (k n) -> p k n", k=KD),
                                     ACT.Copy, scale=1.0 / (X_SCALE * EDGE_SCALE)).then_inc(h_high, 1)
                act.wait_ge(sup_ready, g + 1)
                for r in range(GR):
                    last = nc.scalar.activation(rows(sup, g * GR + r)[:, 0:D], S4[r][:, 0:D], ACT.Copy,
                                                scale=1.0 / (X_SCALE * W0_SCALE))
                last.then_inc(sup_high, 1)

            def stage(i, b):
                nc.scalar.copy(hI[:, b, :, :, :].rearrange("p s k n -> p (s k) n"),
                               hT[:, :, :, bass.ds(i * P, P)].rearrange("p s k n -> p (s k) n")
                               ).then_inc(hi_staged, 1)

            copy_group(0, 0, first=True)
            act.wait_ge(w_loaded, 96)
            nc.scalar.activation(edge16[:, 0, :, :], edge_sb, ACT.Copy, scale=EDGE_SCALE).then_inc(w_high, 1)
            nc.scalar.activation(w0n16[:, 0, :, :], w0n, ACT.Copy, scale=W0_SCALE).then_inc(w_high, 1)
            act.wait_ge(bias_ready, 1)
            nc.scalar.copy(b0_sb[:, :], O[0][:, 0:D])
            nc.scalar.copy(b1_sb[:, :], O[1][:, 0:D]).then_inc(bias_copied, 1)
            act.wait_ge(wt_ready, 1)
            nc.scalar.copy(w1T[:, :, :], S4[0].rearrange("p (k n) -> p k n", k=KD)).then_inc(wt_copied, 1)
            copy_group(1, 1, first=True)
            with act.Fori(0, NG - 3, 2) as g0:
                for b in range(2):
                    high_parts(g0 + b)
                    copy_group(g0 + b + 2, b)
            high_parts(NG - 2)
            act.wait_ge(h_split, 1)
            for i in range(2):
                stage(i, i)
            high_parts(NG - 1)
            act.wait_ge(node_dve, 2)
            nc.scalar.activation(att[:, :], logits[:, :], ACT.Exp, bias=small[:, 2:3], scale=1.0,
                                 accum_out=small[:, 3:4]).then_inc(node_act, 1)

            def mask(i, b, w, first=False):
                if not (first and w < NM):
                    act.wait_ge(e_masked, W * i + w - NM + 1)
                nc.scalar.activation(negs[:, w % NM, :], A16[:, b, w * PC:(w + 1) * PC], ACT.Copy,
                                     bias=NEG_BIG, scale=-NEG_BIG).then_inc(negs_ready, 1)

            def masks(i, b, first=False):
                act.wait_ge(a16_ready, W * (i + 1))
                for w in range(W):
                    mask(i, b, w, first)

            def exps(i, b, w):
                nc.scalar.activation(M[:, b, w * PC:(w + 1) * PC], M[:, b, w * PC:(w + 1) * PC], ACT.Exp,
                                     bias=negmax[:, b:b + 1], scale=1.0,
                                     accum_out=piecesum[:, b, w:w + 1]).then_inc(p_ready, 1)

            def high_part(i, b, w, first=False):
                if w == 0 and not first:
                    act.wait_ge(pt_loaded[0], 16 * i)
                if w >= 1:
                    act.wait_ge(p_split, W * i + w)
                act.wait_ge(p_ready, W * i + w + 1)
                nc.scalar.activation(HL[b][w][:, 0:PC], M[:, b, w * PC:(w + 1) * PC], ACT.Copy, scale=P_SCALE
                                     ).then_inc(p_high, 1)

            def weights(i, b, first=False):
                act.wait_ge(negmax_ready, i + 1)
                exps(i, b, 0)
                for w in range(1, W):
                    exps(i, b, w)
                    high_part(i, b, w - 1, first)
                    if first:
                        mask(i + 1, 1 - b, w - 1)
                high_part(i, b, W - 1)
                if first:
                    mask(i + 1, 1 - b, W - 1)

            def attend(i, b):
                masks(i, b)
                stage(i + 1, 1 - b)
                weights(i, b)

            def high_g(first_row, last_row):
                for j in range(first_row, last_row):
                    nc.scalar.activation(G[:, j, 0:D], x1[:, j, :], ACT.Copy, scale=dscaled[:, j:j + 1]
                                         ).then_inc(g_high, 1)

            masks(0, 0, first=True)
            act.wait_ge(a16_ready, W * 2)
            weights(0, 0, first=True)
            stage(2, 0)
            weights(1, 1)
            with act.Fori(2, NB - 3, 2) as i0:
                for b in range(2):
                    attend(i0 + b, b)
            attend(NB - 2, 0)
            masks(NB - 1, 1)
            weights(NB - 1, 1)
            act.wait_ge(d_ready, 1)
            act.wait_ge(e_ready, W * NB)
            act.wait_ge(row_done, NB - 2)
            high_g(0, NB - 2)
            act.wait_ge(row_done, NB - 1)
            high_g(NB - 2, NB - 1)
            act.wait_ge(row_done, NB)
            high_g(NB - 1, NB)

            def copy_hmT(j):
                act.wait_ge(hmt_ready, j + 1)
                nc.scalar.copy(hmT[:, :, :], HT_BANK[:, 0:D].rearrange("p (k n) -> p k n", k=KD)
                               ).then_inc(hmt_copied, 1)

            def tanh(j):
                act.wait_ge(lin_biased, j + 1)
                nc.scalar.activation(th[:, :], th[:, :], ACT.Tanh).then_inc(tanh_done, 1)

            with act.Fori(0, NB, 1) as j:
                copy_hmT(j)
                tanh(j)

        @block.vector
        def _(dve):
            links = [0]

            def mark(ins):
                links[0] = links[0] + 1
                ins.then_inc(dve_chain, 1)

            def join():
                dve.wait_ge(dve_chain, links[0])

            def link(ins):
                mark(ins)
                join()

            def carry_wait(n):
                nc.vector.memset(scratch[:, n:n + 1], 0.0)

            def rsqrt_seed(v, r):
                link(nc.vector.tensor_scalar(r.bitcast(I32), v.bitcast(I32), -0.5, float(RSQRT_SEED),
                                             ALU.mult, ALU.add))

            def rsqrt_step(v, r, t):
                link(nc.vector.scalar_tensor_tensor(out=t, in0=r, scalar=-0.5, in1=r, op0=ALU.mult, op1=ALU.mult))
                link(nc.vector.tensor_tensor(t, t, v, ALU.mult))
                link(nc.vector.scalar_tensor_tensor(out=r, in0=t, scalar=1.5, in1=r, op0=ALU.add, op1=ALU.mult))

            def check(i, w, first=False):
                h = w // HW
                col = (w % HW) * PC
                if w % HW == 0:
                    dve.wait_ge(a_loaded[h], 16 * (i + 1))
                a = A[:, h, col:col + PC]
                if not (first and w < 2):
                    dve.wait_ge(a_checked, W * i + w - 1)
                nc.vector.scalar_tensor_tensor(
                    out=junk[:, w % 2, :], in0=a, scalar=1.0, in1=a, op0=ALU.is_equal, op1=ALU.not_equal,
                    accum_out=unequal[:, bass.ds(i * W + w, 1)]).then_inc(a_checked, 1)

            def copy_group(g, b):
                dve.wait_ge(xt_high, g + 1)
                nc.vector.scalar_tensor_tensor(
                    out=xT[b][:, 1, :, :], in0=EA.rearrange("p (k n) -> p k n", k=KD), scalar=X_SCALE,
                    in1=xT[b][:, 0, :, :], op0=ALU.mult, op1=ALU.subtract).then_inc(xt_split, 1)

            def low_parts(g):
                dve.wait_ge(h_high, g + 1)
                nc.vector.scalar_tensor_tensor(
                    out=hT[:, 1, :, bass.ds(g * CH, CH)], in0=EB.rearrange("p (k n) -> p k n", k=KD),
                    scalar=1.0 / (X_SCALE * EDGE_SCALE),
                    in1=hT[:, 0, :, bass.ds(g * CH, CH)], op0=ALU.mult, op1=ALU.subtract,
                    accum_out=h_guard[:, bass.ds(g, 1)]).then_inc(h_split, 1)
                dve.wait_ge(sup_high, g + 1)
                for r in range(GR):
                    j = g * GR + r
                    nc.vector.scalar_tensor_tensor(
                        out=rows(sup, j)[:, D:2 * D], in0=S4[r][:, 0:D], scalar=1.0 / (X_SCALE * W0_SCALE),
                        in1=rows(sup, j)[:, 0:D],
                        op0=ALU.mult, op1=ALU.subtract, accum_out=sup_guard[:, bass.ds(j, 1)])
                    last = nc.vector.tensor_scalar(logits[:, bass.ds(j, 1)], S4[r][:, D:D + 1],
                                                   1.0 / (X_SCALE * W0_SCALE), None, ALU.mult)
                last.then_inc(sup_split, 1)

            copy_group(0, 0)
            for n, (halves, whole, scale) in enumerate(((edge16, edge_sb, EDGE_SCALE), (w0n16, w0n, W0_SCALE))):
                dve.wait_ge(w_high, n + 1)
                nc.vector.scalar_tensor_tensor(out=halves[:, 1, :, :], in0=whole, scalar=scale,
                                               in1=halves[:, 0, :, :], op0=ALU.mult, op1=ALU.subtract
                                               ).then_inc(w_split, 1)
            copy_group(1, 1)
            for g in range(NG):
                low_parts(g)
                check(g // W, g % W, first=(g < W))
                if g + 2 < NG:
                    copy_group(g + 2, g % 2)

            dve.wait_ge(sup_split, NG)
            nc.vector.tensor_reduce(small[:, 0:1], logits[:, :], AX.X, ALU.max).then_inc(node_dve, 1)
            dve.wait_ge(node_pool, 1)
            nc.vector.tensor_scalar(small[:, 2:3], small[:, 1:2], -1.0, None, ALU.mult).then_inc(node_dve, 1)

            def mask_and_max(i, b, w, first=False):
                dve.wait_ge(negs_ready, W * i + w + 1)
                dve.wait_ge(e_ready, W * i + w + 1)
                if not first:
                    if w + 1 < W:
                        dve.wait_ge(pt_loaded[w + 1], 16 * (i - 1))
                    else:
                        dve.wait_ge(p_split, W * (i - 1))
                carry_wait(w)
                nc.vector.tensor_tensor_reduce(
                    out=M[:, b, w * PC:(w + 1) * PC], in0=E[w % NE], in1=negs[:, w % NM, :], scale=1.0,
                    scalar=-3.0e38, op0=ALU.add, op1=ALU.max, accum_out=piecemax[:, w:w + 1]
                ).then_inc(e_masked, 1)

            def row_max(i, b):
                dve.wait_ge(e_masked, W * i + W)
                nc.vector.tensor_reduce(negmax[:, b:b + 1], piecemax[:, :], AX.X, ALU.max, negate=True
                                        ).then_inc(negmax_ready, 1)

            def low_part(i, b, w):
                dve.wait_ge(p_high, W * i + w + 1)
                nc.vector.scalar_tensor_tensor(out=HL[b][w][:, PC:2 * PC], in0=M[:, b, w * PC:(w + 1) * PC],
                                               scalar=P_SCALE, in1=HL[b][w][:, 0:PC],
                                               op0=ALU.mult, op1=ALU.subtract).then_inc(p_split, 1)

            def moments_1():
                mark(nc.vector.bn_stats(stats[:, :], y[:, :]))

            def moments_2():
                join()
                carry_wait(W)
                mark(nc.vector.bn_aggr(meanvar[:, :], stats[:, :]))

            def moments_3():
                join()
                mark(nc.vector.tensor_scalar(nv[:, 0:1], meanvar[:, 1:2], EPS, None, ALU.add))
                mark(nc.vector.tensor_scalar(nvh[:, :], meanvar[:, 1:2], EPS, -0.5, ALU.add, ALU.mult))

            def variance_seed():
                join()
                mark(nc.vector.tensor_scalar(ny[:, 0:1].bitcast(I32), nv[:, 0:1].bitcast(I32), -0.5,
                                             float(RSQRT_SEED), ALU.mult, ALU.add))

            def variance_step_1():
                join()
                mark(nc.vector.scalar_tensor_tensor(out=nt[:, 0:1], in0=ny[:, 0:1], scalar=nvh[:, :],
                                                    in1=ny[:, 0:1], op0=ALU.mult, op1=ALU.mult))

            def variance_step_2():
                join()
                mark(nc.vector.scalar_tensor_tensor(out=ny[:, 0:1], in0=nt[:, 0:1], scalar=1.5,
                                                    in1=ny[:, 0:1], op0=ALU.add, op1=ALU.mult))

            def normalise(dst):
                join()
                return nc.vector.tensor_scalar(dst, y[:, :], meanvar[:, 0:1], ny[:, 0:1], ALU.subtract, ALU.mult)

            def moments_and_rsqrt():
                moments_1()
                moments_2()
                moments_3()
                variance_seed()
                for _ in range(RSQRT_STEPS):
                    variance_step_1()
                    variance_step_2()

            def row_scale_1(b):
                mark(nc.vector.tensor_reduce(rowscale[:, 0:1], piecesum[:, b, :], AX.X, ALU.add))
                mark(nc.vector.tensor_scalar(rowscale[:, 3:4], negmax[:, b:b + 1], -0.5 * NEG_BIG, 1.0 / P_SCALE,
                                             ALU.is_lt, ALU.mult))

            def row_scale_2():
                join()
                mark(nc.vector.reciprocal(rowscale[:, 1:2], rowscale[:, 0:1]))

            def row_scale_3(i):
                join()
                mark(nc.vector.scalar_tensor_tensor(out=rowscale[:, 2:3], in0=rowscale[:, 1:2],
                                                    scalar=rowscale[:, 3:4], in1=att[:, bass.ds(i, 1)],
                                                    op0=ALU.mult, op1=ALU.mult))

            def residual_1(i, b):
                dve.wait_ge(pv_done, W * (i + 1))
                dve.wait_ge(x_biased, i + 1)
                join()
                mark(nc.vector.scalar_tensor_tensor(out=y2[:, :], in0=O[b][:, D:2 * D], scalar=rowscale[:, 2:3],
                                                    in1=rows(x1, i), op0=ALU.mult, op1=ALU.add))

            def residual_2(i, b, first=False):
                if not first:
                    dve.wait_ge(row_done, i)
                join()
                nc.vector.scalar_tensor_tensor(out=y[:, :], in0=O[b][:, 0:D], scalar=rowscale[:, 2:3],
                                               in1=y2[:, :], op0=ALU.mult, op1=ALU.add).then_inc(o_read, 1)
                dve.wait_ge(o_read, i + 1)

            def finish_row(i):
                normalise(rows(x1, i)).then_inc(row_done, 1)

            for w in range(W):
                mask_and_max(0, 0, w, first=True)
            row_max(0, 0)
            dve.wait_ge(node_pool, 2)
            link(nc.vector.reciprocal(small[:, 5:6], small[:, 4:5]))
            link(nc.vector.tensor_scalar(att[:, :], att[:, :], small[:, 5:6], None, ALU.mult))

            def step(i, b, before=2, last=False):
                o = 1 - b
                if before == 0:
                    low_part(0, 0, 0)
                mask_and_max(i + 1, o, 0, first=(before == 0))
                if before:
                    residual_1(i - 1, o)
                else:
                    low_part(0, 0, 1)
                mask_and_max(i + 1, o, 1, first=(before == 0))
                if before:
                    residual_2(i - 1, o, first=(before == 1))
                else:
                    low_part(0, 0, 2)
                mask_and_max(i + 1, o, 2, first=(before == 0))
                if before:
                    moments_1()
                else:
                    low_part(0, 0, 3)
                mask_and_max(i + 1, o, 3, first=(before == 0))
                row_max(i + 1, o)
                if before:
                    moments_2()
                if not last:
                    check(i + 2, 0)
                row_scale_1(b)
                if before:
                    moments_3()
                if not last:
                    check(i + 2, 1)
                row_scale_2()
                if before:
                    variance_seed()
                    variance_step_1()
                low_part(i + 1, o, 0)
                row_scale_3(i)
                if before:
                    variance_step_2()
                if last:
                    degree_step(0)
                else:
                    check(i + 2, 2)
                if before:
                    variance_step_1()
                low_part(i + 1, o, 1)
                if before:
                    variance_step_2()
                if last:
                    degree_step(1)
                else:
                    check(i + 2, 3)
                if before:
                    variance_step_1()
                low_part(i + 1, o, 2)
                if before:
                    variance_step_2()
                if last:
                    degree_step(2)
                low_part(i + 1, o, 3)
                if before:
                    finish_row(i - 1)
                if last:
                    degree_step(3)
                    degree_step(4)

            def degree_step(n):
                degree = (deg[:, :], dinv[:, :], dt[:, :])
                if n == 0:
                    dve.wait_ge(deg_ready, 1)
                    link(nc.vector.tensor_scalar(deg[:, :], HT_BANK[:, 0:NB], 1.0, None, ALU.add))
                    rsqrt_seed(*degree[:2])
                elif 1 <= n <= RSQRT_STEPS:
                    rsqrt_step(*degree)
                elif n == RSQRT_STEPS + 1:
                    nc.vector.tensor_scalar(dscaled[:, :], dinv[:, :], G_SCALE, None, ALU.mult).then_inc(d_ready, 1)
                    link(nc.vector.tensor_scalar(dunscaled[:, :], dinv[:, :], 1.0 / G_SCALE, None, ALU.mult))

            step(0, 0, before=0)
            marks = links[0]
            step(1, 1, before=1)
            per_step = links[0] - marks
            with dve.Fori(2, NB - 3, 2) as i0:
                for b in range(2):
                    links[0] = marks + per_step * (i0 + b - 1)
                    step(i0 + b, b)
            links[0] = marks + per_step * (NB - 3)
            step(NB - 2, 0, last=True)

            def low_g(first_row, last_row):
                for j in range(first_row, last_row):
                    dve.wait_ge(g_high, j + 1)
                    nc.vector.scalar_tensor_tensor(out=G[:, j, D:2 * D], in0=x1[:, j, :], scalar=dscaled[:, j:j + 1],
                                                   in1=G[:, j, 0:D], op0=ALU.mult, op1=ALU.subtract
                                                   ).then_inc(g_split, 1)

            def end_of_block(i, b, g):
                residual_1(i, b)
                low_g(g, g + 1)
                residual_2(i, b)
                low_g(g + 1, g + 2)
                moments_1()
                low_g(g + 2, g + 3)
                moments_2()
                low_g(g + 3, g + 4)
                moments_3()
                low_g(g + 4, g + 5)
                variance_seed()
                low_g(g + 5, g + 6)
                for n in range(RSQRT_STEPS):
                    variance_step_1()
                    low_g(g + 6 + 2 * n, g + 7 + 2 * n)
                    variance_step_2()
                    low_g(g + 7 + 2 * n, g + 8 + 2 * n)
                finish_row(i)
                return g + 6 + 2 * RSQRT_STEPS

            g = end_of_block(NB - 2, 0, 0)
            row_scale_1(1)
            low_g(g, g + 1)
            row_scale_2()
            low_g(g + 1, g + 2)
            row_scale_3(NB - 1)
            g = end_of_block(NB - 1, 1, g + 2)
            low_g(g, NB)

            dve.wait_ge(a_checked, W * NB)
            link(nc.vector.tensor_reduce(guard[:, 0:1], unequal[:, :], AX.X, ALU.max))
            link(nc.vector.tensor_reduce(guard[:, 1:2], h_guard[:, :], AX.X, ALU.add))
            link(nc.vector.tensor_reduce(guard[:, 2:3], sup_guard[:, :], AX.X, ALU.add))
            link(nc.vector.tensor_reduce(guard[:, 3:4], logits[:, :], AX.X, ALU.add))
            link(nc.vector.tensor_tensor(guard[:, 1:2], guard[:, 1:2], guard[:, 2:3], ALU.add))
            link(nc.vector.tensor_tensor(guard[:, 3:4], guard[:, 1:2], guard[:, 3:4], ALU.add))
            link(nc.vector.tensor_scalar(guard[:, 3:4], guard[:, 3:4], 0.0, 0.0, ALU.mult, ALU.is_equal))
            link(nc.vector.tensor_scalar(guard[:, 0:1], guard[:, 0:1], 0.0, 1.0, ALU.is_gt, ALU.add))
            nc.vector.tensor_tensor(guard[:, 4:5], guard[:, 0:1], guard[:, 3:4], ALU.subtract).then_inc(bad_rows, 1)

            def scale_rows(j, b, first=False):
                dve.wait_ge(ag_done, j + 1)
                link(nc.vector.scalar_tensor_tensor(out=y2[:, :], in0=rows(x1, j),
                                                    scalar=dscaled[:, bass.ds(j, 1)], in1=O[b][:, 0:D],
                                                    op0=ALU.mult, op1=ALU.add))
                nc.vector.tensor_tensor(y2[:, :], y2[:, :], O[b][:, D:2 * D], ALU.add).then_inc(o2_read, 1)
                if not first:
                    dve.wait_ge(hmt_ready, j)
                dve.wait_ge(o2_read, j + 1)
                nc.vector.tensor_scalar(hm[:, :], y2[:, :], dunscaled[:, bass.ds(j, 1)], None, ALU.mult
                                        ).then_inc(hm_ready, 1)

            def add_b1(j):
                dve.wait_ge(lin_ready, j + 1)
                nc.vector.tensor_tensor(th[:, :], LIN_BANK[:, 0:D], b1_sb[:, :], ALU.add).then_inc(lin_biased, 1)

            def tail(j, b, early=2):
                dve.wait_ge(tanh_done, j + 1)
                if early >= 1:
                    dve.wait_ge(y_ready, j)
                if early >= 2:
                    dve.wait_ge(stored[b], 8 * (j - b))
                link(nc.vector.tensor_tensor(y[:, :], th[:, :], rows(x1, j), ALU.add))
                moments_and_rsqrt()
                normalise(obuf[:, b, :]).then_inc(y_ready, 1)

            def second_layer(j, b, early=2):
                scale_rows(j, b)
                tail(j - 1, 1 - b, early)
                add_b1(j)

            scale_rows(0, 0, first=True)
            add_b1(0)
            second_layer(1, 1, early=0)
            before2 = links[0]
            second_layer(2, 0, early=1)
            per_block = links[0] - before2
            with dve.Fori(3, NB - 2, 2) as j0:
                for b in range(2):
                    links[0] = before2 + per_block * (j0 + b - 2)
                    second_layer(j0 + b, 1 - b)
            links[0] = before2 + per_block * (NB - 3)
            second_layer(NB - 1, 1)
            tail(NB - 1, 1)

            dve.wait_ge(bad_all, 1)
            nc.vector.tensor_copy(flag[:, :], guard[:, 5:6]).then_inc(flag_ready, 1)
            dve.wait_ge(flag_ready, 1)


def general_path(nc, flag, x, adj, w0, b0, node_w, edge_w, w1, b1, out):
    N, D = x.shape
    NB = N // P
    KD = D // P
    CH = 512
    UN = CH
    U = N // UN
    C = N // CH
    TJ = CH // P
    GR = CH // P
    NG = NB // GR

    with ExitStack() as ctx:
        def sb(name, shape, dt=F32):
            return ctx.enter_context(nc.sbuf_tensor(name, shape, dt))

        def psum(name, shape, dt=F32):
            return ctx.enter_context(nc.psum_tensor(name, shape, dt))

        def sem(name):
            return ctx.enter_context(nc.semaphore(name))

        hT = sb("hT", [P, KD, N])
        sup = sb("sup", [P, NB, D])
        x1 = sb("x1", [P, NB, D])
        A = sb("A", [P, 2, N])
        M = sb("M", [P, 2, N])
        colsum = sb("colsum", [P, N])
        negs = sb("negs", [P, 2, CH])
        PT = sb("PT", [P, 4, CH])
        hI = sb("hI", [P, 2, KD, P])
        edge_sb = sb("edge_sb", [P, KD, D])
        w0n = sb("w0n", [P, KD, D + 1])
        w1T = sb("w1T", [P, KD, D])
        b0_sb = sb("b0_sb", [P, D])
        b1_sb = sb("b1_sb", [P, D])
        ident = sb("ident", [P, P])
        ones = sb("ones", [P, P])
        logits = sb("logits", [P, NB])
        att = sb("att", [P, NB])
        small = sb("small", [P, 8])
        unitmax = sb("unitmax", [P, U])
        negmax = sb("negmax", [P, 2])
        unitsum = sb("unitsum", [P, 2, U])
        rowscale = sb("rowscale", [P, 4])
        stats = sb("stats", [P, 6])
        meanvar = sb("meanvar", [P, 2])
        nv = sb("nv", [P, NB])
        ny = sb("ny", [P, NB])
        nt = sb("nt", [P, NB])
        dinv = sb("dinv", [P, NB])
        scratch = sb("scratch", [P, 1])
        y = sb("y", [P, D])
        hm = sb("hm", [P, D])
        hmT = sb("hmT", [P, KD, P])
        th = sb("th", [P, D])
        obuf = sb("obuf", [P, 2, D])
        w1_sb = obuf
        b0_row, b1_row = y[0:1, :], hm[0:1, :]
        xg = [A[:, b, 0:GR * D].rearrange("p (r d) -> p r d", r=GR) for b in range(2)]
        xT = [M[:, b, 0:KD * CH].rearrange("p (k n) -> p k n", k=KD) for b in range(2)]

        E4 = psum("E4", [P, 4 * CH])
        E = [E4[:, i * CH:(i + 1) * CH] for i in range(4)]
        EA, EB = E4[:, 0:2 * CH], E4[:, 2 * CH:4 * CH]
        T = [psum(f"T{i}", [P, CH]) for i in range(2)]
        O = [psum(f"O{i}", [P, CH]) for i in range(2)]
        S4 = T + O

        w_loaded = sem("w_loaded")
        x1_loaded = sem("x1_loaded")
        xg_loaded = [sem(f"xg_loaded{i}") for i in range(2)]
        a_loaded = [sem(f"a_loaded{i}") for i in range(2)]
        ident_zero = sem("ident_zero")
        consts = sem("consts")
        bias_ready = sem("bias_ready")
        bias_copied = sem("bias_copied")
        wt_ready = sem("wt_ready")
        wt_copied = sem("wt_copied")
        xt_ready = sem("xt_ready")
        xt_copied_act = sem("xt_copied_act")
        xt_copied_dve = sem("xt_copied_dve")
        h_ready = sem("h_ready")
        h_copied = sem("h_copied")
        sup_ready = sem("sup_ready")
        sup_copied = sem("sup_copied")
        node_dve = sem("node_dve")
        node_pool = sem("node_pool")
        node_act = sem("node_act")
        att_ready = sem("att_ready")
        hi_staged = sem("hi_staged")
        x_biased = sem("x_biased")
        a_summed = sem("a_summed")
        a_used = sem("a_used")
        e_ready = sem("e_ready")
        e_masked = sem("e_masked")
        negmax_ready = sem("negmax_ready")
        exp_done = sem("exp_done")
        p_ready = sem("p_ready")
        t_ready = sem("t_ready")
        t_copied = sem("t_copied")
        pv_done = sem("pv_done")
        o_read = sem("o_read")
        deg_ready = sem("deg_ready")
        g_ready = sem("g_ready")
        hm_ready = sem("hm_ready")
        hmt_ready = sem("hmt_ready")
        hmt_copied = sem("hmt_copied")
        lin_ready = sem("lin_ready")
        lin_biased = sem("lin_biased")
        tanh_done = sem("tanh_done")
        y_ready = sem("y_ready")
        stored = [sem(f"stored{i}") for i in range(2)]
        dve_chain = sem("dve_chain")

        x_groups = x.rearrange("(g r p) d -> g p r d", p=P, r=GR)
        x_rows = x.rearrange("(b p) d -> p b d", p=P)
        adj_rows = adj.rearrange("(b p) n -> b p n", p=P)
        out_rows = out.rearrange("(b p) d -> b p d", p=P)

        block = ctx.enter_context(nc.Block())

        @block.sync
        def _(sp):
            with sp.If(sp.value_load(flag[0:1, 0:1], min_val=0, max_val=1) != 0):
                sp.dma_start(edge_sb[:, :, :], edge_w.rearrange("(k p) d -> p k d", p=P)).then_inc(w_loaded, 16)
                sp.dma_start(w0n[:, :, 0:D], w0.rearrange("(k p) d -> p k d", p=P)).then_inc(w_loaded, 16)
                sp.dma_start(w0n[:, :, D:D + 1], node_w.rearrange("(k p) d -> p k d", p=P),
                             allow_slow_non_contiguous=True).then_inc(w_loaded, 16)
                sp.dma_start(w1_sb[:, :, :], w1.rearrange("(k p) d -> p k d", p=P)).then_inc(w_loaded, 16)
                sp.dma_start(b0_row[:, :], b0.rearrange("(a d) -> a d", a=1)).then_inc(w_loaded, 16)
                sp.dma_start(b1_row[:, :], b1.rearrange("(a d) -> a d", a=1)).then_inc(w_loaded, 16)
                for g in range(2):
                    sp.dma_start(xg[g], x_groups[g]).then_inc(xg_loaded[g], 16)
                with sp.Fori(2, NG - 1, 2) as g0:
                    for b in range(2):
                        g = g0 + b
                        sp.wait_ge(xt_ready, g - 1)
                        sp.dma_start(xg[b], x_groups[bass.ds(g, 1)].rearrange("a p r d -> (a p) r d")
                                     ).then_inc(xg_loaded[b], 16)
                sp.dma_start(x1[:, :, :], x_rows).then_inc(x1_loaded, 16)
                sp.wait_ge(xt_ready, NG)
                for b in range(2):
                    sp.dma_start(A[:, b, :], adj_rows[b]).then_inc(a_loaded[b], 16)
                with sp.Fori(2, NB - 1, 2) as i0:
                    for b in range(2):
                        i = i0 + b
                        sp.wait_ge(a_used, i - 1)
                        sp.wait_ge(a_summed, i - 1)
                        sp.dma_start(A[:, b, :], adj_rows[bass.ds(i, 1)].rearrange("a p n -> (a p) n")
                                     ).then_inc(a_loaded[b], 16)
                for b in range(2):
                    sp.wait_ge(a_used, NB - 1 + b)
                    sp.wait_ge(a_summed, NB - 1 + b)
                    sp.dma_start(A[:, b, :], adj_rows[b]).then_inc(a_loaded[b], 16)
                with sp.Fori(0, NB - 3, 2) as j0:
                    for b in range(2):
                        j = j0 + b
                        sp.wait_ge(t_ready, C * (NB + 1) + C * j)
                        sp.dma_start(A[:, b, :], adj_rows[bass.ds(j + 2, 1)].rearrange("a p n -> (a p) n")
                                     ).then_inc(a_loaded[b], 16)
                        sp.wait_ge(y_ready, j + 1)
                        sp.dma_start(out_rows[bass.ds(j, 1)].rearrange("a p d -> (a p) d"), obuf[:, b, :]
                                     ).then_inc(stored[b], 16)
                for b in range(2):
                    sp.wait_ge(y_ready, NB - 1 + b)
                    sp.dma_start(out_rows[NB - 2 + b], obuf[:, b, :]).then_inc(stored[b], 16)
                for b in range(2):
                    sp.wait_ge(stored[b], 16 * (NB // 2))

        @block.tensor
        def _(pe):
            with pe.If(pe.value_load(flag[0:1, 0:1], min_val=0, max_val=1) != 0):
                pe.wait_ge(consts, 3)
                pe.wait_ge(w_loaded, 96)
                nc.tensor.matmul(O[0][:, 0:D], ones[0:1, :], b0_row[:, :], start=True, stop=True)
                nc.tensor.matmul(O[1][:, 0:D], ones[0:1, :], b1_row[:, :], start=True, stop=True
                                 ).then_inc(bias_ready, 1)
                for k in range(KD):
                    for o in range(KD):
                        last = nc.tensor.transpose(T[0][:, (k * KD + o) * P:(k * KD + o + 1) * P],
                                                   w1_sb[:, o, k * P:(k + 1) * P], ident[:, :])
                last.then_inc(wt_ready, 1)

                def transpose_group(g, b):
                    pe.wait_ge(xg_loaded[b], 8 * (g - b) + 16)
                    for k in range(KD):
                        for r in range(GR):
                            last = nc.tensor.transpose(EA[:, k * CH + r * P:k * CH + (r + 1) * P],
                                                       xg[b][:, r, k * P:(k + 1) * P], ident[:, :])
                    last.then_inc(xt_ready, 1)

                def project_group(g, b, first=False):
                    pe.wait_ge(xt_copied_act, g + 1)
                    pe.wait_ge(xt_copied_dve, g + 1)
                    if not first:
                        pe.wait_ge(h_copied, g)
                    for m in range(KD):
                        for k in range(KD):
                            last = nc.tensor.matmul(EB[:, m * CH:(m + 1) * CH], edge_sb[:, k, m * P:(m + 1) * P],
                                                    xT[b][:, k, :], start=(k == 0), stop=(k == KD - 1))
                    last.then_inc(h_ready, 1)
                    if not first:
                        pe.wait_ge(sup_copied, g)
                    for r in range(GR):
                        for k in range(KD):
                            last = nc.tensor.matmul(S4[r][:, 0:D + 1], xT[b][:, k, r * P:(r + 1) * P], w0n[:, k, :],
                                                    start=(k == 0), stop=(k == KD - 1))
                    last.then_inc(sup_ready, 1)

                def next_transpose(g, b):
                    pe.wait_ge(xt_copied_act, g)
                    pe.wait_ge(xt_copied_dve, g)
                    transpose_group(g, b)

                transpose_group(0, 0)
                pe.wait_ge(bias_copied, 1)
                pe.wait_ge(wt_copied, 1)
                next_transpose(1, 1)
                project_group(0, 0, first=True)
                next_transpose(2, 0)
                project_group(1, 1)
                with pe.Fori(2, NG - 3, 2) as g0:
                    for b in range(2):
                        next_transpose(g0 + b + 1, (b + 1) % 2)
                        project_group(g0 + b, b)
                next_transpose(NG - 1, 1)
                project_group(NG - 2, 0)
                project_group(NG - 1, 1)

                def scores(i, b, first=False):
                    pe.wait_ge(hi_staged, i + 1)
                    for u in range(U):
                        if not (first and u < 4):
                            pe.wait_ge(e_masked, U * i + u - 3)
                        for k in range(KD):
                            last = nc.tensor.matmul(E[u % 4], hI[:, b, k, :], hT[:, k, u * UN:(u + 1) * UN],
                                                    start=(k == 0), stop=(k == KD - 1))
                        last.then_inc(e_ready, 1)

                def transpose_chunk(n, c, src, first=False):
                    if not (first and c < 2):
                        pe.wait_ge(t_copied, C * n + c - 1)
                    for t in range(TJ):
                        col = c * CH + t * P
                        last = nc.tensor.transpose(T[c % 2][:, t * P:(t + 1) * P], src[:, col:col + P], ident[:, :])
                    last.then_inc(t_ready, 1)

                def product_chunk(n, b, c):
                    pe.wait_ge(t_copied, C * n + c + 1)
                    for t in range(TJ):
                        last = nc.tensor.matmul(O[b][:, 0:D], PT[:, c % 4, t * P:(t + 1) * P], sup[:, c * TJ + t, :],
                                                start=(c == 0 and t == 0), stop=(c == C - 1 and t == TJ - 1))
                    last.then_inc(pv_done, 1)

                def attend(i, b, first=False):
                    for c in range(C):
                        pe.wait_ge(p_ready, U * i + c + 1)
                        transpose_chunk(i, c, M[:, b, :], first)
                        if c == 1 and not first:
                            pe.wait_ge(o_read, i - 1)
                        if c > 0:
                            product_chunk(i, b, c - 1)
                    product_chunk(i, b, C - 1)

                pe.wait_ge(h_copied, NG)
                pe.wait_ge(sup_copied, NG)
                scores(0, 0, first=True)
                scores(1, 1)
                attend(0, 0, first=True)
                scores(2, 0)
                attend(1, 1)
                with pe.Fori(2, NB - 3, 2) as i0:
                    for b in range(2):
                        scores(i0 + b + 1, (b + 1) % 2)
                        attend(i0 + b, b)
                scores(NB - 1, 1)
                attend(NB - 2, 0)
                attend(NB - 1, 1)

                pe.wait_ge(a_summed, NB)
                for t in range(NB):
                    last = nc.tensor.matmul(E[0][:, t:t + 1], colsum[:, t * P:(t + 1) * P], ones[:, 0:1],
                                            start=True, stop=True)
                last.then_inc(deg_ready, 1)

                def hm_transpose(j):
                    pe.wait_ge(hm_ready, j + 1)
                    for k in range(KD):
                        last = nc.tensor.transpose(E[0][:, k * P:(k + 1) * P], hm[:, k * P:(k + 1) * P], ident[:, :])
                    last.then_inc(hmt_ready, 1)

                def hm_linear(j):
                    pe.wait_ge(hmt_copied, j + 1)
                    pe.wait_ge(lin_biased, j)
                    for k in range(KD):
                        last = nc.tensor.matmul(E[1][:, 0:D], hmT[:, k, :], w1T[:, k, :],
                                                start=(k == 0), stop=(k == KD - 1))
                    last.then_inc(lin_ready, 1)

                def aggregate(j, b, first=False):
                    n = NB + j
                    pe.wait_ge(a_loaded[b], 16 * (NB // 2) + 8 * (j - b) + 16)
                    for c in range(C):
                        transpose_chunk(n, c, A[:, b, :])
                        if c == 1:
                            pe.wait_ge(o_read, n - 1)
                        if c > 0:
                            if first:
                                pe.wait_ge(g_ready, TJ * c)
                            product_chunk(n, b, c - 1)
                        if c == 3 and not first:
                            hm_transpose(j - 1)
                        if c == 5 and not first:
                            hm_linear(j - 1)
                    if first:
                        pe.wait_ge(g_ready, NB)
                    product_chunk(n, b, C - 1)

                aggregate(0, 0, first=True)
                aggregate(1, 1)
                with pe.Fori(2, NB - 1, 2) as j0:
                    for b in range(2):
                        aggregate(j0 + b, b)
                hm_transpose(NB - 1)
                hm_linear(NB - 1)

        @block.gpsimd
        def _(pool):
            with pool.If(pool.value_load(flag[0:1, 0:1], min_val=0, max_val=1) != 0):
                nc.gpsimd.memset(ident[:, :], 0.0).then_inc(ident_zero, 1)
                nc.gpsimd.memset(ones[:, :], 1.0).then_inc(consts, 1)
                pool.wait_ge(ident_zero, 1)
                nc.gpsimd.affine_select(out=ident[:, :], in_=ident[:, :], compare_op=ALU.not_equal, fill=1.0, base=0,
                                        pattern=[[-1, P]], channel_multiplier=1).then_inc(consts, 1)
                nc.gpsimd.memset(colsum[:, :], 0.0).then_inc(consts, 1)
                pool.wait_ge(bias_copied, 1)
                pool.wait_ge(x1_loaded, 16)
                pool.wait_ge(h_copied, NG)

                def stage(i, b):
                    nc.gpsimd.tensor_copy(hI[:, b, :, :], hT[:, :, bass.ds(i * P, P)]).then_inc(hi_staged, 1)

                def add_bias(i):
                    nc.gpsimd.tensor_tensor(x1[:, bass.ds(i, 1), :].rearrange("p a d -> p (a d)"),
                                            x1[:, bass.ds(i, 1), :].rearrange("p a d -> p (a d)"), b0_sb[:, :],
                                            ALU.add).then_inc(x_biased, 1)

                def add_columns(i, b, first=False):
                    pool.wait_ge(a_loaded[b], 8 * (i - b) + 16)
                    if not first:
                        pool.wait_ge(a_summed, i)
                    nc.gpsimd.tensor_tensor(colsum[:, :], colsum[:, :], A[:, b, :], ALU.add).then_inc(a_summed, 1)

                stage(0, 0)
                stage(1, 1)
                pool.wait_ge(node_dve, 1)
                nc.gpsimd.partition_all_reduce(small[:, 1:2], small[:, 0:1], P, RMAX).then_inc(node_pool, 1)
                pool.wait_ge(node_act, 1)
                nc.gpsimd.partition_all_reduce(small[:, 4:5], small[:, 3:4], P, RADD).then_inc(node_pool, 1)
                pool.wait_ge(consts, 3)
                add_bias(0)
                add_columns(0, 0, first=True)
                add_bias(1)
                add_columns(1, 1)
                with pool.Fori(2, NB - 1, 2) as i0:
                    for b in range(2):
                        i = i0 + b
                        pool.wait_ge(e_ready, U * (i - 1))
                        stage(i, b)
                        add_bias(i)
                        add_columns(i, b)

        @block.scalar
        def _(act):
            with act.If(act.value_load(flag[0:1, 0:1], min_val=0, max_val=1) != 0):
                act.wait_ge(bias_ready, 1)
                nc.scalar.copy(b0_sb[:, :], O[0][:, 0:D])
                nc.scalar.copy(b1_sb[:, :], O[1][:, 0:D]).then_inc(bias_copied, 1)
                act.wait_ge(wt_ready, 1)
                nc.scalar.copy(w1T[:, :, :], T[0][:, :].rearrange("p (k n) -> p k n", k=KD)).then_inc(wt_copied, 1)

                def copy_group(g, b, first=False):
                    act.wait_ge(xt_ready, g + 1)
                    if not first:
                        act.wait_ge(sup_ready, g - 1)
                    nc.scalar.copy(xT[b][:, 0, :], EA[:, 0:CH]).then_inc(xt_copied_act, 1)

                def copy_h(g):
                    act.wait_ge(h_ready, g + 1)
                    nc.scalar.copy(hT[:, :, bass.ds(g * CH, CH)], EB.rearrange("p (k n) -> p k n", k=KD)
                                   ).then_inc(h_copied, 1)

                copy_group(0, 0, first=True)
                copy_group(1, 1, first=True)
                with act.Fori(0, NG - 3, 2) as g0:
                    for b in range(2):
                        copy_h(g0 + b)
                        copy_group(g0 + b + 2, b)
                copy_h(NG - 2)
                copy_h(NG - 1)
                act.wait_ge(node_dve, 2)
                nc.scalar.activation(att[:, :], logits[:, :], ACT.Exp, bias=small[:, 2:3], scale=1.0,
                                     accum_out=small[:, 3:4]).then_inc(node_act, 1)

                def exps(i, b, u):
                    if u == 0:
                        act.wait_ge(negmax_ready, i + 1)
                    nc.scalar.activation(M[:, b, u * UN:(u + 1) * UN], M[:, b, u * UN:(u + 1) * UN], ACT.Exp,
                                         bias=negmax[:, b:b + 1], scale=1.0,
                                         accum_out=unitsum[:, b, u:u + 1]).then_inc(exp_done, 1)

                def copy_transposed(n, c, first=False):
                    act.wait_ge(t_ready, C * n + c + 1)
                    if not (first and c < 4):
                        act.wait_ge(pv_done, C * n + c - 3)
                    nc.scalar.copy(PT[:, c % 4, :], T[c % 2][:, :]).then_inc(t_copied, 1)

                def attend(i, b, first=False, last=False):
                    for c in range(C):
                        copy_transposed(i, c, first)
                        if not last:
                            exps(i + 1, (b + 1) % 2, c)

                for u in range(U):
                    exps(0, 0, u)
                attend(0, 0, first=True)
                attend(1, 1)
                with act.Fori(2, NB - 3, 2) as i0:
                    for b in range(2):
                        attend(i0 + b, b)
                attend(NB - 2, 0)
                attend(NB - 1, 1, last=True)

                def aggregate(j, first=False):
                    for c in range(C):
                        copy_transposed(NB + j, c)
                        if c == 4 and not first:
                            copy_hmT(j - 1)
                        if c == 7 and not first:
                            tanh(j - 1)

                def copy_hmT(j):
                    act.wait_ge(hmt_ready, j + 1)
                    nc.scalar.copy(hmT[:, :, :], E[0][:, 0:D].rearrange("p (k n) -> p k n", k=KD)
                                   ).then_inc(hmt_copied, 1)

                def tanh(j):
                    act.wait_ge(lin_biased, j + 1)
                    nc.scalar.activation(th[:, :], th[:, :], ACT.Tanh).then_inc(tanh_done, 1)

                aggregate(0, first=True)
                with act.Fori(1, NB, 1) as j:
                    aggregate(j)
                copy_hmT(NB - 1)
                tanh(NB - 1)

        @block.vector
        def _(dve):
            with dve.If(dve.value_load(flag[0:1, 0:1], min_val=0, max_val=1) != 0):
                links = [0]

                def link(ins):
                    links[0] = links[0] + 1
                    ins.then_inc(dve_chain, 1)
                    dve.wait_ge(dve_chain, links[0])

                def carry_wait():
                    nc.vector.memset(scratch[:, :], 0.0)

                def rsqrt(v, r, t):
                    link(nc.vector.tensor_scalar(r.bitcast(I32), v.bitcast(I32), -0.5, float(RSQRT_SEED),
                                                 ALU.mult, ALU.add))
                    for _ in range(RSQRT_STEPS):
                        link(nc.vector.scalar_tensor_tensor(out=t, in0=r, scalar=-0.5, in1=r, op0=ALU.mult,
                                                            op1=ALU.mult))
                        link(nc.vector.tensor_tensor(t, t, v, ALU.mult))
                        link(nc.vector.scalar_tensor_tensor(out=r, in0=t, scalar=1.5, in1=r, op0=ALU.add,
                                                            op1=ALU.mult))

                def copy_group(g, b, first=False):
                    dve.wait_ge(xt_ready, g + 1)
                    if not first:
                        dve.wait_ge(sup_ready, g - 1)
                    nc.vector.tensor_copy(xT[b][:, 1, :], EA[:, CH:2 * CH]).then_inc(xt_copied_dve, 1)

                def copy_support(g):
                    dve.wait_ge(sup_ready, g + 1)
                    for r in range(GR):
                        nc.vector.tensor_copy(sup[:, bass.ds(g * GR + r, 1), :].rearrange("p a d -> p (a d)"),
                                              S4[r][:, 0:D])
                        last = nc.vector.tensor_copy(logits[:, bass.ds(g * GR + r, 1)], S4[r][:, D:D + 1])
                    last.then_inc(sup_copied, 1)

                copy_group(0, 0, first=True)
                copy_group(1, 1, first=True)
                with dve.Fori(0, NG - 3, 2) as g0:
                    for b in range(2):
                        copy_support(g0 + b)
                        copy_group(g0 + b + 2, b)
                copy_support(NG - 2)
                copy_support(NG - 1)

                def mask_and_max(i, b):
                    dve.wait_ge(a_loaded[b], 8 * (i - b) + 16)
                    def mask(u):
                        return nc.vector.tensor_scalar(negs[:, u % 2, :], A[:, b, u * UN:(u + 1) * UN], 0.0, NEG_BIG,
                                                       ALU.is_le, ALU.mult)

                    dve.wait_ge(e_masked, U * i)
                    ins = mask(0)
                    for u in range(U):
                        link(ins)
                        dve.wait_ge(e_ready, U * i + u + 1)
                        dve.wait_ge(e_masked, U * i + u)
                        if u + 1 < U:
                            ins = mask(u + 1)
                        else:
                            carry_wait()
                        nc.vector.tensor_tensor_reduce(
                            out=M[:, b, u * UN:(u + 1) * UN], in0=E[u % 4], in1=negs[:, u % 2, :], scale=1.0,
                            scalar=-3.0e38, op0=ALU.add, op1=ALU.max, accum_out=unitmax[:, u:u + 1]
                        ).then_inc(e_masked, 1)
                    dve.wait_ge(e_masked, U * i + U)
                    nc.vector.tensor_reduce(negmax[:, b:b + 1], unitmax[:, :], AX.X, ALU.max, negate=True
                                            ).then_inc(negmax_ready, 1)

                def weigh(i, b):
                    for u in range(U):
                        dve.wait_ge(exp_done, U * i + u + 1)
                        cols = slice(u * UN, (u + 1) * UN)
                        ins = nc.vector.tensor_tensor(M[:, b, cols], M[:, b, cols], A[:, b, cols], ALU.mult)
                        ins.then_inc(p_ready, 1)
                    dve.wait_ge(p_ready, U * i + U)
                    nc.vector.sem_inc(a_used, 1)

                def normalise(dst):
                    link(nc.vector.bn_stats(stats[:, :], y[:, :]))
                    carry_wait()
                    link(nc.vector.bn_aggr(meanvar[:, :], stats[:, :]))
                    link(nc.vector.tensor_scalar(nv[:, 0:1], meanvar[:, 1:2], EPS, None, ALU.add))
                    rsqrt(nv[:, 0:1], ny[:, 0:1], nt[:, 0:1])
                    return nc.vector.tensor_scalar(dst, y[:, :], meanvar[:, 0:1], ny[:, 0:1], ALU.subtract, ALU.mult)

                def finish_first(i, b):
                    link(nc.vector.tensor_reduce(rowscale[:, 0:1], unitsum[:, b, :], AX.X, ALU.add))
                    link(nc.vector.reciprocal(rowscale[:, 1:2], rowscale[:, 0:1]))
                    link(nc.vector.tensor_tensor(rowscale[:, 2:3], rowscale[:, 1:2], att[:, bass.ds(i, 1)], ALU.mult))
                    dve.wait_ge(pv_done, C * (i + 1))
                    dve.wait_ge(x_biased, i + 1)
                    row = x1[:, bass.ds(i, 1), :].rearrange("p a d -> p (a d)")
                    nc.vector.scalar_tensor_tensor(out=y[:, :], in0=O[b][:, 0:D], scalar=rowscale[:, 2:3], in1=row,
                                                   op0=ALU.mult, op1=ALU.add).then_inc(o_read, 1)
                    dve.wait_ge(o_read, i + 1)
                    link(normalise(row))

                dve.wait_ge(sup_copied, NG)
                nc.vector.tensor_reduce(small[:, 0:1], logits[:, :], AX.X, ALU.max).then_inc(node_dve, 1)
                dve.wait_ge(node_pool, 1)
                nc.vector.tensor_scalar(small[:, 2:3], small[:, 1:2], -1.0, None, ALU.mult).then_inc(node_dve, 1)
                dve.wait_ge(node_pool, 2)
                link(nc.vector.reciprocal(small[:, 5:6], small[:, 4:5]))
                link(nc.vector.tensor_scalar(att[:, :], att[:, :], small[:, 5:6], None, ALU.mult))

                mask_and_max(0, 0)
                weigh(0, 0)

                def step(i, b):
                    mask_and_max(i + 1, (b + 1) % 2)
                    weigh(i + 1, (b + 1) % 2)
                    finish_first(i, b)

                step(0, 0)
                before = links[0]
                step(1, 1)
                per_step = links[0] - before
                with dve.Fori(2, NB - 3, 2) as i0:
                    for b in range(2):
                        links[0] = before + per_step * (i0 + b - 1)
                        step(i0 + b, b)
                links[0] = before + per_step * (NB - 3)
                step(NB - 2, 0)
                finish_first(NB - 1, 1)

                dve.wait_ge(deg_ready, 1)
                link(nc.vector.tensor_scalar(nv[:, :], E[0][:, 0:NB], 1.0, None, ALU.add))
                rsqrt(nv[:, :], ny[:, :], nt[:, :])
                link(nc.vector.tensor_scalar(nt[:, :], nv[:, :], 0.0, None, ALU.not_equal))
                link(nc.vector.tensor_tensor(dinv[:, :], ny[:, :], nt[:, :], ALU.mult))
                with dve.Fori(0, NB, 1) as j:
                    nc.vector.tensor_scalar(sup[:, bass.ds(j, 1), :].rearrange("p a d -> p (a d)"),
                                            x1[:, bass.ds(j, 1), :].rearrange("p a d -> p (a d)"),
                                            dinv[:, bass.ds(j, 1)], None, ALU.mult).then_inc(g_ready, 1)
                dve.wait_ge(g_ready, NB)

                def scale_rows(j, b):
                    dve.wait_ge(pv_done, C * (NB + 1) + C * j)
                    dve.wait_ge(y_ready, j)
                    g = sup[:, bass.ds(j, 1), :].rearrange("p a d -> p (a d)")
                    nc.vector.tensor_tensor(y[:, :], O[b][:, 0:D], g, ALU.add).then_inc(o_read, 1)
                    dve.wait_ge(o_read, NB + j + 1)
                    nc.vector.tensor_scalar(hm[:, :], y[:, :], dinv[:, bass.ds(j, 1)], None, ALU.mult
                                            ).then_inc(hm_ready, 1)

                def bias_linear(j):
                    dve.wait_ge(lin_ready, j + 1)
                    nc.vector.tensor_tensor(th[:, :], E[1][:, 0:D], b1_sb[:, :], ALU.add).then_inc(lin_biased, 1)

                def finish_second(j, b, first=False):
                    dve.wait_ge(tanh_done, j + 1)
                    if not first:
                        dve.wait_ge(stored[b], 8 * (j - b))
                    row = x1[:, bass.ds(j, 1), :].rearrange("p a d -> p (a d)")
                    link(nc.vector.tensor_tensor(y[:, :], th[:, :], row, ALU.add))
                    normalise(obuf[:, b, :]).then_inc(y_ready, 1)

                def tail(j, b, first=False):
                    bias_linear(j)
                    finish_second(j, b, first)

                scale_rows(0, 0)
                tail(0, 0, first=True)
                scale_rows(1, 1)
                before2 = links[0]
                tail(1, 1, first=True)
                per_tail = links[0] - before2
                with dve.Fori(2, NB - 1, 2) as j0:
                    for b in range(2):
                        scale_rows(j0 + b, b)
                        links[0] = before2 + per_tail * (j0 + b - 1)
                        tail(j0 + b, b)


def build(nc, x, adj, w0, b0, node_w, edge_w, w1, b1, out):
    adj16 = nc.dram_tensor("adj16", adj.shape, F16).ap()
    with nc.sbuf_tensor("flag", [P, 1], I32) as flag:
        split_path(nc, flag, adj16, x, adj, w0, b0, node_w, edge_w, w1, b1, out)
        general_path(nc, flag, x, adj, w0, b0, node_w, edge_w, w1, b1, out)


_INS = ['x', 'adj', 'L0_gnn_weight', 'L0_gnn_bias', 'L0_gnn_node_w', 'L0_gnn_edge_w', 'L1_gnn_W', 'L1_gnn_b']
_OUTS = [((4096, 256), 'float32')]


def kernel(**inputs):
    import numpy as _np
    import concourse.bacc as _bacc
    from concourse import mybir as _mybir
    from concourse.bass_utils import run_bass_kernel_spmd as _run

    nc = _bacc.Bacc("TRN2", target_bir_lowering=False, num_devices=1)
    arrays, args = {}, []
    for name in _INS:
        a = _np.ascontiguousarray(inputs[name])
        arrays[f"in_{name}_dram"] = a
        args.append(nc.dram_tensor(f"in_{name}_dram", a.shape, _mybir.dt.from_np(a.dtype), kind="ExternalInput").ap())
    for i, (shape, dtype) in enumerate(_OUTS):
        dt = _mybir.dt.from_np(_np.dtype(dtype))
        args.append(nc.dram_tensor(f"out_{i}_dram", shape, dt, kind="ExternalOutput").ap())
    build(nc, *args)
    r = _run(nc, [arrays], core_ids=[0])
    got = tuple(r.results[0][f"out_{i}_dram"] for i in range(len(_OUTS)))
    return got[0]
```
